# Optimizing a Trainium2 kernel written in Bass

```python
import numpy as np
import jax
import jax.numpy as jnp

def _softmax(x, axis=-1):
    return jax.nn.softmax(x, axis=axis)

def _gelu(x):
    return jax.nn.gelu(x, approximate=True)

def _silu(x):
    return jax.nn.silu(x)

def _sigmoid(x):
    return jax.nn.sigmoid(x)

def _layernorm(x, axis=-1, eps=1e-05):
    m = jnp.mean(x, axis=axis, keepdims=True)
    v = jnp.var(x, axis=axis, keepdims=True)
    return (x - m) / jnp.sqrt(v + eps)

def _scatter_add(tgt, idx, src, axis=0):
    return tgt.at[idx].add(src)

def _segment_sum(src, seg, n):
    return jax.ops.segment_sum(src, seg, n)
kernel_name = 'mk_macaron_d1_jaxref_r8_73179f'

def setup_inputs(seed: int=0):
    np.random.seed(seed)
    _w = jnp.asarray

    def _L0_attn_setup():
        import jax, jax.numpy as jnp
        import numpy as np
        B, N, D, H = (4, 512, 128, 16)
        HD = D // H
        MLP = 4 * D

        def _ln(x, w, b):
            m = x.mean(-1, keepdims=True)
            v = x.var(-1, keepdims=True)
            return (x - m) / jnp.sqrt(v + 1e-05) * w + b
        key = jax.random.key(seed)
        ks = jax.random.split(key, 12)
        s = 1.0 / np.sqrt(D)
        sm = 1.0 / np.sqrt(MLP)
        return {'q_x': jax.random.normal(ks[0], (B, N, D), jnp.float32), 'ln1_w': jnp.ones((D,), jnp.float32), 'ln1_b': jnp.zeros((D,), jnp.float32), 'wq': jax.random.normal(ks[1], (D, D), jnp.float32) * s, 'bq': jnp.zeros((D,), jnp.float32), 'wk': jax.random.normal(ks[2], (D, D), jnp.float32) * s, 'bk': jnp.zeros((D,), jnp.float32), 'wv': jax.random.normal(ks[3], (D, D), jnp.float32) * s, 'bv': jnp.zeros((D,), jnp.float32), 'wo': jax.random.normal(ks[4], (D, D), jnp.float32) * s, 'bo': jnp.zeros((D,), jnp.float32), 'ln2_w': jnp.ones((D,), jnp.float32), 'ln2_b': jnp.zeros((D,), jnp.float32), 'fc_w': jax.random.normal(ks[5], (D, MLP), jnp.float32) * s, 'fc_b': jnp.zeros((MLP,), jnp.float32), 'proj_w': jax.random.normal(ks[6], (MLP, D), jnp.float32) * sm, 'proj_b': jnp.zeros((D,), jnp.float32)}
    _L0_attn_in = _L0_attn_setup()

    def _L0_ffn_setup():
        import jax, jax.numpy as jnp
        import numpy as np
        B, S, D, H, E, K, F = (1, 128, 128, 16, 8, 2, 512)

        def layernorm(x, g, b, eps=1e-05):
            m = x.mean(-1, keepdims=True)
            v = ((x - m) ** 2).mean(-1, keepdims=True)
            return (x - m) * jax.lax.rsqrt(v + eps) * g + b
        key = jax.random.key(seed)
        ks = jax.random.split(key, 8)
        n = lambda k, shape, sc: jax.random.normal(k, shape, dtype=jnp.float32) * sc
        return {'x': n(ks[0], (B, S, D), 1.0), 'w_qkv': n(ks[1], (D, 3 * D), D ** (-0.5)), 'w_o': n(ks[2], (D, D), D ** (-0.5)), 'g1': jnp.ones((D,), jnp.float32), 'b1': jnp.zeros((D,), jnp.float32), 'wg': n(ks[3], (D, E), D ** (-0.5)), 'w1': n(ks[4], (E, D, F), D ** (-0.5)), 'bb1': jnp.zeros((E, F), jnp.float32), 'w2': n(ks[5], (E, F, D), F ** (-0.5)), 'bb2': jnp.zeros((E, D), jnp.float32), 'g2': jnp.ones((D,), jnp.float32), 'b2': jnp.zeros((D,), jnp.float32)}
    _L0_ffn_in = _L0_ffn_setup()
    _d = {'L0_attn_q_x': _L0_attn_in['q_x'], 'L0_attn_ln1_w': _L0_attn_in['ln1_w'], 'L0_attn_ln1_b': _L0_attn_in['ln1_b'], 'L0_attn_wq': _L0_attn_in['wq'], 'L0_attn_bq': _L0_attn_in['bq'], 'L0_attn_wk': _L0_attn_in['wk'], 'L0_attn_bk': _L0_attn_in['bk'], 'L0_attn_wv': _L0_attn_in['wv'], 'L0_attn_bv': _L0_attn_in['bv'], 'L0_attn_wo': _L0_attn_in['wo'], 'L0_attn_bo': _L0_attn_in['bo'], 'L0_attn_ln2_w': _L0_attn_in['ln2_w'], 'L0_attn_ln2_b': _L0_attn_in['ln2_b'], 'L0_attn_fc_w': _L0_attn_in['fc_w'], 'L0_attn_fc_b': _L0_attn_in['fc_b'], 'L0_attn_proj_w': _L0_attn_in['proj_w'], 'L0_attn_proj_b': _L0_attn_in['proj_b'], 'L0_ffn_w_qkv': _L0_ffn_in['w_qkv'], 'L0_ffn_w_o': _L0_ffn_in['w_o'], 'L0_ffn_g1': _L0_ffn_in['g1'], 'L0_ffn_b1': _L0_ffn_in['b1'], 'L0_ffn_wg': _L0_ffn_in['wg'], 'L0_ffn_w1': _L0_ffn_in['w1'], 'L0_ffn_bb1': _L0_ffn_in['bb1'], 'L0_ffn_w2': _L0_ffn_in['w2'], 'L0_ffn_bb2': _L0_ffn_in['bb2'], 'L0_ffn_g2': _L0_ffn_in['g2'], 'L0_ffn_b2': _L0_ffn_in['b2']}
    _x0 = _d['L0_attn_q_x']
    _d['L0_attn_q_x'] = jax.random.normal(jax.random.fold_in(jax.random.key(seed), 1), (4, 1024, 128), dtype=_x0.dtype)
    del _x0
    return _d

def reference(L0_attn_q_x, L0_attn_ln1_w, L0_attn_ln1_b, L0_attn_wq, L0_attn_bq, L0_attn_wk, L0_attn_bk, L0_attn_wv, L0_attn_bv, L0_attn_wo, L0_attn_bo, L0_attn_ln2_w, L0_attn_ln2_b, L0_attn_fc_w, L0_attn_fc_b, L0_attn_proj_w, L0_attn_proj_b, L0_ffn_w_qkv, L0_ffn_w_o, L0_ffn_g1, L0_ffn_b1, L0_ffn_wg, L0_ffn_w1, L0_ffn_bb1, L0_ffn_w2, L0_ffn_bb2, L0_ffn_g2, L0_ffn_b2):

    def _L0_attn_ref(q_x, ln1_w, ln1_b, wq, bq, wk, bk, wv, bv, wo, bo, ln2_w, ln2_b, fc_w, fc_b, proj_w, proj_b):
        import jax, jax.numpy as jnp
        import numpy as np
        B, N, D, H = (4, 512, 128, 16)
        HD = D // H
        MLP = 4 * D

        def _ln(x, w, b):
            m = x.mean(-1, keepdims=True)
            v = x.var(-1, keepdims=True)
            return (x - m) / jnp.sqrt(v + 1e-05) * w + b
        b, n, c = q_x.shape
        xn = _ln(q_x, ln1_w, ln1_b)
        q = (xn @ wq + bq).reshape(b, n, H, HD).transpose(0, 2, 1, 3)
        k = (xn @ wk + bk).reshape(b, n, H, HD).transpose(0, 2, 1, 3)
        v = (xn @ wv + bv).reshape(b, n, H, HD).transpose(0, 2, 1, 3)
        fq = jax.nn.elu(q) + 1.0
        fk = jax.nn.elu(k) + 1.0
        kv = jnp.einsum('bhnd,bhne->bnde', fk, v)
        qkv = jnp.einsum('bhnd,bnde->bhne', fq, kv)
        k_sum = fk.sum(axis=1)
        qk = jnp.einsum('bhnd,bnd->bhn', fq, k_sum)
        attn = qkv / (qk[..., None] + 1e-06)
        attn = attn.transpose(0, 2, 1, 3).reshape(b, n, c)
        attn = attn @ wo + bo
        x = q_x + attn
        h = _ln(x, ln2_w, ln2_b)
        h = jax.nn.gelu(h @ fc_w + fc_b, approximate=False)
        return x + (h @ proj_w + proj_b)

    def _L0_ffn_ref(x, w_qkv, w_o, g1, b1, wg, w1, bb1, w2, bb2, g2, b2):
        import jax, jax.numpy as jnp
        import numpy as np
        B, S, D, H, E, K, F = (1, 128, 128, 16, 8, 2, 512)

        def layernorm(x, g, b, eps=1e-05):
            m = x.mean(-1, keepdims=True)
            v = ((x - m) ** 2).mean(-1, keepdims=True)
            return (x - m) * jax.lax.rsqrt(v + eps) * g + b
        b, s, d = x.shape
        hd = d // H
        qkv = x @ w_qkv
        q, k, v = jnp.split(qkv, 3, axis=-1)
        to_heads = lambda t: t.reshape(b, s, H, hd).transpose(0, 2, 1, 3)
        q, k, v = (to_heads(q), to_heads(k), to_heads(v))
        scores = jnp.einsum('bhqd,bhkd->bhqk', q, k) / jnp.sqrt(jnp.float32(hd))
        causal = jnp.tril(jnp.ones((s, s), bool))
        scores = jnp.where(causal, scores, jnp.finfo(scores.dtype).min)
        attn = jax.nn.softmax(scores, axis=-1)
        o = jnp.einsum('bhqk,bhkd->bhqd', attn, v)
        o = o.transpose(0, 2, 1, 3).reshape(b, s, d) @ w_o
        h = layernorm(x + o, g1, b1)
        probs = jax.nn.softmax(h @ wg, axis=-1)
        topv, topi = jax.lax.top_k(probs, K)
        topv = topv / topv.sum(-1, keepdims=True)
        w = (topv[..., None] * jax.nn.one_hot(topi, E, dtype=h.dtype)).sum(-2)
        h1 = jax.nn.gelu(jnp.einsum('bsd,edf->ebsf', h, w1) + bb1[:, None, None, :])
        y = jnp.einsum('ebsf,efd->ebsd', h1, w2) + bb2[:, None, None, :]
        moe = jnp.einsum('ebsd,bse->bsd', y, w)
        return layernorm(h + moe, g2, b2)
    x = L0_attn_q_x
    x = x + 0.5 * _L0_ffn_ref(_layernorm(x, axis=-1), L0_ffn_w_qkv, L0_ffn_w_o, L0_ffn_g1, L0_ffn_b1, L0_ffn_wg, L0_ffn_w1, L0_ffn_bb1, L0_ffn_w2, L0_ffn_bb2, L0_ffn_g2, L0_ffn_b2)
    x = x + _L0_attn_ref(_layernorm(x, axis=-1), L0_attn_ln1_w, L0_attn_ln1_b, L0_attn_wq, L0_attn_bq, L0_attn_wk, L0_attn_bk, L0_attn_wv, L0_attn_bv, L0_attn_wo, L0_attn_bo, L0_attn_ln2_w, L0_attn_ln2_b, L0_attn_fc_w, L0_attn_fc_b, L0_attn_proj_w, L0_attn_proj_b)
    x = x + 0.5 * _L0_ffn_ref(_layernorm(x, axis=-1), L0_ffn_w_qkv, L0_ffn_w_o, L0_ffn_g1, L0_ffn_b1, L0_ffn_wg, L0_ffn_w1, L0_ffn_bb1, L0_ffn_w2, L0_ffn_bb2, L0_ffn_g2, L0_ffn_b2)
    return x

_drawn_inputs = setup_inputs


def setup_inputs(seed=0):
    import zlib

    import numpy as np

    out = dict(_drawn_inputs(seed))
    spreads = {'L0_attn_ln1_w': (1.0, 0.555),
     'L0_attn_ln1_b': (0.0, 0.619),
     'L0_attn_bq': (0.0, 2.0),
     'L0_attn_bk': (0.0, 0.8),
     'L0_attn_bv': (0.0, 0.675),
     'L0_attn_bo': (0.0, 0.1),
     'L0_attn_ln2_w': (1.0, 0.2),
     'L0_attn_ln2_b': (0.0, 0.1),
     'L0_attn_fc_b': (0.0, 0.274),
     'L0_attn_proj_b': (0.0, 0.1),
     'L0_ffn_g1': (1.0, 0.2),
     'L0_ffn_b1': (0.0, 0.1),
     'L0_ffn_bb1': (0.0, 0.357),
     'L0_ffn_bb2': (0.0, 0.1),
     'L0_ffn_g2': (1.0, 0.2),
     'L0_ffn_b2': (0.0, 0.1)}
    factors = {'L0_attn_wq': 2.781}
    for name, (base, spread) in spreads.items():
        noise = np.random.default_rng([zlib.crc32(name.encode()), seed]).standard_normal(out[name].shape)
        drawn = base * np.exp(spread * noise) if base else spread * noise
        out[name] = jnp.asarray(drawn.astype(out[name].dtype))
    for name, factor in factors.items():
        out[name] = (out[name] * factor).astype(out[name].dtype)
    return out
```

```python
import math
from contextlib import ExitStack

import concourse.bass as bass
import numpy as np
from concourse import mybir
from concourse.alu_op_type import AluOpType as ALU

F32 = mybir.dt.float32
F32R = mybir.dt.float32r
BF16 = mybir.dt.bfloat16
ACT = mybir.ActivationFunctionType
AX = mybir.AxisListType

B, N, D, H = 4, 1024, 128, 16
HD = D // H
E, F = 8, 512
P = 128
TB = N // P
NT = B * TB
G4 = 4
NG = H // G4
STRIP = P // G4
FC = F // P
EPS = 1e-5
NEG = -1e30
SCALE = 1.0 / math.sqrt(HD)
BANK = 512
BIG_LOADS = 2 * E + 1 + 3 + 1 + 1 + 1 + 5
ONE_ROW = 3 * HD
QUAD = NT // 4


def next_uses(first):
    uses = [("Q", 0, 0, 1131), ("K", 0, 0, 1131)]
    if not first:
        uses.append(("MT", 1, -1, 620))
    uses.append(("V", 0, 0, 350))
    low = [("S", i, hp, 2 * (i + 1) * P / 0.96 + 65) for i in range(4) for hp in range(2)]
    high = [("S", i, h, (i + 1) * P / 0.96 + 65) for i in range(4, TB) for h in range(G4)]
    return uses + low + high[:2] + [("MT", 0, 0, 620)] + high[2:]


def current_uses(closing):
    groups = [(0, j) for j in range(4)] + [(1, j) for j in range(TB)]
    out = []
    for n, (half, j) in enumerate(groups):
        width = BANK - P * max(0, j - 4 * half)
        out.append(("ST", half, j, G4 * (width / 1.2 + 52)))
        if n:
            out.append(("PV", *groups[n - 1], 0))
        if n == 5:
            out.append(("OT", 0, 0, 0))
    out.append(("PV", *groups[-1], 0))
    return out


def merge(a, b):
    out, ta, tb, i, j = [], 0.0, 0.0, 0, 0
    sa, sb = sum(x[3] for x in a) or 1, sum(x[3] for x in b) or 1
    while i < len(a) or j < len(b):
        if j == len(b) or (i < len(a) and ta / sa <= tb / sb):
            out.append(a[i]); ta += a[i][3]; i += 1
        else:
            out.append(b[j]); tb += b[j][3]; j += 1
    return out


def attention_schedule(last):
    out, u = [], 0
    for g in range(NG):
        cur = current_uses(False)
        if g:
            cur.insert(2, ("OT", 1, -1, 0))
        nxt = [] if last and g == NG - 1 else next_uses(False)
        if not nxt:
            nxt = [("MT", 1, -1, 620)]
        items = merge(nxt, cur)
        if g == NG - 1:
            items.append(("OT", 1, 0, 0))
        for kind, x, y, _ in items:
            du = kind in ("Q", "K", "V", "S", "MT", "OT")
            out.append((g, kind, x, y, u if du else None))
            u += du
    return out, u


PROLOGUE = [(0, kind, x, y, u) for u, (kind, x, y, _) in enumerate(next_uses(True))]
BODY, BODY_USES = attention_schedule(False)
LAST_BODY, LAST_USES = attention_schedule(True)
assert BODY_USES % 2 == 0
EXPS = NG * 12 * G4
assert EXPS % 3 == 0 and EXPS % 8 == 0


def program(nc, q_x, ln1_w, ln1_b, wq, bq, wk, bk, wv, bv, wo, bo, ln2_w, ln2_b, fc_w, fc_b, proj_w, proj_b,
            w_qkv, w_o, g1, b1, wg, w1, bb1, w2, bb2, g2, b2, consts, out):
    with ExitStack() as ctx:
        def sb(name, shape, dt=F32):
            return ctx.enter_context(nc.sbuf_tensor("sb_" + name, shape, dt))

        def sem(name):
            return ctx.enter_context(nc.semaphore(name))

        x = sb("x", [P, NT, D])
        xn = sb("xn", [P, NT, D])
        o = sb("o", [P, NT, D])
        ft = sb("ft", [P, NT * P])
        wr = sb("wr", [P, NT, E])

        cst = sb("cst", [P, 3 * P + 4])
        ident = cst[:, 0:P]
        coef_k, coef_q, bias_k = (cst[:, 3 * P + i:3 * P + i + 1] for i in range(3))
        identb = sb("identb", [P, P], BF16)
        maskb = sb("maskb", [P, 2, P], BF16)

        wqkv = sb("wqkv", [P, 3 * D])
        wqk = sb("wqk", [P, NG, 2, P])
        w_o_s = sb("w_o_s", [P, D])
        wg_s = sb("wg_s", [P, E])
        w1s = sb("w1s", [P, E, F])
        w2s = sb("w2s", [P, E, FC, D])
        by_feature = sb("by_feature", [E * FC + 2, P])
        fcols = sb("fcols", [P, E * FC + 2])
        bb2s = sb("bb2s", [E, D])
        rows = sb("rows", [P, 4, D])

        wall = sb("wall", [P, 3 * D])
        wo_s = sb("wo_s", [P, D])
        fc_s = sb("fc_s", [P, F])
        pj_s = sb("pj_s", [P, FC, D])
        by_feature2 = sb("by_feature2", [4 + FC, P])
        mcols = sb("mcols", [P, 4 + FC])
        mrows = sb("mrows", [P, 5 * D])

        ps = ctx.enter_context(nc.psum_tensor("ps", [P, 8 * BANK], F32))

        def bank(i, n=BANK, k=1):
            return ps[:, i * BANK:i * BANK + n]

        x_dram = q_x.rearrange("b (t p) d -> p (b t) d", p=P)
        s_x, s_w, s_c, s_prep = sem("x_loaded"), sem("w_loaded"), sem("c_loaded"), sem("prepared")
        s_big = sem("expert_weights_loaded")
        with nc.Block() as block:
            @block.sync
            def _(sp):
                for b in range(B):
                    sp.dma_start(x[:, b * TB:(b + 1) * TB, :], x_dram[:, b * TB:(b + 1) * TB, :]).then_inc(s_x, 16)
                for e in range(E):
                    sp.dma_start(w1s[:, e, :], w1[e]).then_inc(s_big, 16)
                    sp.dma_start(w2s[:, e, :, :], w2[e].rearrange("(c p) d -> p c d", p=P)).then_inc(s_big, 16)
                sp.dma_start(bb2s[:, :], bb2).then_inc(s_big, 16)
                for i, w in enumerate((wq, wk, wv)):
                    sp.dma_start(wall[:, i * D:(i + 1) * D], w).then_inc(s_big, 16)
                sp.dma_start(wo_s[:, :], wo).then_inc(s_big, 16)
                sp.dma_start(fc_s[:, :], fc_w).then_inc(s_big, 16)
                sp.dma_start(pj_s[:, :, :], proj_w.rearrange("(c p) d -> p c d", p=P)).then_inc(s_big, 16)
                for i, row in enumerate((bq, bk, bv, bo, proj_b)):
                    sp.dma_start(mrows[:, i * D:(i + 1) * D], row.rearrange("(a d) -> a d", a=1).to_broadcast([P, D])).then_inc(s_big, 16)

            @block.scalar
            def _(act):
                act.dma_start(cst[:, :], consts).then_inc(s_c, 16)
                act.dma_start(wqkv[:, :], w_qkv).then_inc(s_w, 16)
                act.dma_start(w_o_s[:, :], w_o).then_inc(s_w, 16)
                act.dma_start(wg_s[:, :], wg).then_inc(s_w, 16)
                act.dma_start(by_feature[0:E * FC, :], bb1.rearrange("e (c p) -> (e c) p", p=P)).then_inc(s_w, 16)
                for i, row in enumerate((g1, b1)):
                    act.dma_start(by_feature[E * FC + i:E * FC + i + 1, :], row.rearrange("(a d) -> a d", a=1)).then_inc(s_w, 16)
                for i, row in enumerate((ln1_w, ln1_b, ln2_w, ln2_b)):
                    act.dma_start(by_feature2[i:i + 1, :], row.rearrange("(a d) -> a d", a=1)).then_inc(s_w, 16)
                act.dma_start(by_feature2[4:4 + FC, :], fc_b.rearrange("(c p) -> c p", p=P)).then_inc(s_w, 16)
                for i, row in enumerate((g1, b1, g2, b2)):
                    act.dma_start(rows[:, i, :], row.rearrange("(a d) -> a d", a=1).to_broadcast([P, D])).then_inc(s_w, 16)

            @block.vector
            def _(dve):
                dve.wait_ge(s_c, 16)
                nc.vector.tensor_copy(identb[:, :], ident)
                nc.vector.tensor_copy(maskb[:, :, :], cst[:, P:3 * P].rearrange("p (a k) -> p a k", a=2))
                nc.vector.memset(wqk[:, :, :, :], 0.0).then_inc(s_prep, 1)
                dve.wait_ge(s_prep, 1)
                dve.wait_ge(s_w, 16 * 15)
                for g in range(NG):
                    for qk in range(2):
                        src = wqkv[:, qk * D + g * 32:qk * D + g * 32 + 32].rearrange("p (j c) -> p j c", j=G4)
                        dst = wqk[:, g, qk, :].rearrange("p (j c) -> p j c", j=G4)
                        for r in range(3):
                            nc.vector.tensor_copy(dst[:, :, r * HD:(r + 1) * HD], src)
                nc.vector.tensor_scalar(rows[:, 2:4, :], rows[:, 2:4, :], 0.5, None, ALU.mult)
                dve.wait_ge(s_prep, 2)
                nc.vector.tensor_copy(fcols[:, :], bank(0, E * FC + 2))
                nc.vector.tensor_copy(mcols[:, :], bank(1, 4 + FC)).then_inc(s_prep, 1)

            @block.tensor
            def _(pe):
                pe.wait_ge(s_c, 16)
                pe.wait_ge(s_w, 16 * 15)
                pe.wait_ge(s_prep, 1)
                nc.tensor.transpose(bank(1, 4 + FC), by_feature2[:, :], cst[0:4 + FC, 0:4 + FC])
                nc.tensor.transpose(bank(0, E * FC + 2), by_feature[:, :], cst[0:E * FC + 2, 0:E * FC + 2]).then_inc(s_prep, 1)

        st6 = sb("st6", [P, 4, 6])
        mv = sb("mv", [P, 2, 4, 2])
        ve = sb("ve", [P, 2, 4])
        sd = sb("sd", [P, 2, 4])

        def stats(dve, source, par):
            for t in range(4):
                nc.vector.bn_stats(st6[:, t, :], source(t))
            dve.drain()
            for t in range(4):
                nc.vector.bn_aggr(mv[:, par, t, :], st6[:, t, :])
            dve.drain()
            return nc.vector.tensor_scalar(ve[:, par, :], mv[:, par, :, 1], EPS, None, ALU.add)

        def credit(eng, *sems):
            for s in sems:
                eng.sem_inc(s, 2)

        def now(eng, s, n):
            eng.wait_ge(s, n + 3)

        def before(eng, s, n):
            eng.wait_ge(s, n + 1)

        def quads(eng, body):
            with eng.Fori(0, QUAD // 2) as i:
                body(i * 2)

        def tiles(t, n):
            return t[:, bass.ds(n * 4, 4), :]

        def tile(t, n, k):
            return t[:, bass.ds(n * 4 + k, 1), :].rearrange("p a d -> p (a d)")

        def wide(row):
            return row.rearrange("p (a d) -> p a d", a=1).to_broadcast([P, 4, row.shape[-1]])

        def quad(i):
            return bank(i).rearrange("p (a d) -> p a d", a=4)

        def turn(i, source):
            for t in range(4):
                last = nc.tensor.transpose(ps[:, i * BANK + t * P:i * BANK + (t + 1) * P], source(t), ident)
            return last

        def normalise(dve, par, out_tile, in_tile):
            nc.vector.reciprocal(ve[:, par, :], sd[:, par, :])
            dve.drain()
            for t in range(4):
                last = nc.vector.tensor_scalar(out_tile(t), in_tile(t), mv[:, par, t, 0:1], ve[:, par, t:t + 1],
                                               ALU.subtract, ALU.mult)
            return last

        def ffn(tag):
            first_norm(tag)
            attention(tag)
            after_attention(tag)
            route(tag)
            experts(tag)

        def attention(tag):
            with ExitStack() as mine:
                attention_of(tag, mine)

        def attention_of(tag, mine):
            def own(name, shape, dt=F32):
                return mine.enter_context(nc.sbuf_tensor(f"{tag}_{name}", shape, dt))

            xt = own("xt", [P, N])
            rnd = own("rnd", [P, 2, N], F32R)
            qa0 = own("qa0", [P, 2, N], F32R)
            qa1 = own("qa1", [P, 2, N], F32R)
            ka = own("ka", [P, 2, N], F32R)
            va = own("va", [P, 2, TB, G4, STRIP])
            mcat = own("mcat", [P, TB, P])
            pt = own("pt", [P, 8, BANK])
            ot = own("ot", [P, 2, BANK])
            rs = own("rs", [P, 2, 4, G4])
            du_full, du_done = sem(f"{tag}_unit_full"), sem(f"{tag}_unit_done")
            rounded = sem(f"{tag}_rounded")
            eu_full, eu_done = sem(f"{tag}_scores_full"), sem(f"{tag}_exp_done")
            pv_done, ov_full, ov_done = sem(f"{tag}_pv_done"), sem(f"{tag}_sum_full"), sem(f"{tag}_sum_out")
            xt_ready, ones = sem(f"{tag}_xt_ready"), sem(f"{tag}_ones")
            PRO = len(PROLOGUE)

            def unit(u0, u):
                return (u0 + u) % 2

            def passes(eng, walk):
                walk(PROLOGUE, 0, 0, None)
                with eng.Fori(0, B - 1) as b:
                    walk(BODY, b * BODY_USES + PRO, PRO, b)
                walk(LAST_BODY, (B - 1) * BODY_USES + PRO, PRO, B - 1)

            def where(sched):
                return {(g, kind, x, y): u for g, kind, x, y, u in sched if u is not None}

            def counts(b):
                return (0, 0, 0) if b is None else (b * EXPS, b * (EXPS // 4), b * (2 * NG))

            with nc.Block() as block:
                @block.tensor
                def _(pe):
                    pe.sem_inc(pv_done, 2)

                    def walk(sched, base, u0, b):
                        at = where(sched)
                        e0, q0, m0 = counts(b)
                        e = q = m = m_ot = 0
                        for g, kind, x, y, u in sched:
                            nxt = (g + 1) % 2 if b is not None else 0
                            gn = (g + 1) % NG if b is not None else 0
                            if u is not None:
                                r = unit(u0, u)
                                if b is not None or u >= 2:
                                    pe.wait_ge(du_done, base + u - 1)
                                lo = r * 2 * BANK
                            if kind in ("Q", "K"):
                                if kind == "Q" and (b is None or g == NG - 1):
                                    pe.wait_ge(xt_ready, 1 if b is None else b + 2)
                                for c in range(2):
                                    last = nc.tensor.matmul(ps[:, lo + c * BANK:lo + (c + 1) * BANK],
                                                            wqk[:, gn, "QK".index(kind), :], xt[:, c * BANK:(c + 1) * BANK],
                                                            start=True, stop=True)
                                last.then_inc(du_full, 1)
                            elif kind == "V":
                                for t in range(TB):
                                    last = nc.tensor.matmul(ps[:, lo + t * STRIP:lo + (t + 1) * STRIP],
                                                            xt[:, t * P:(t + 1) * P],
                                                            wqkv[:, 2 * D + gn * 32:2 * D + gn * 32 + 32],
                                                            start=True, stop=True)
                                last.then_inc(du_full, 1)
                            elif kind == "S":
                                i, width = x, (x + 1) * P
                                pe.wait_ge(du_done, base + at[(g, "V", 0, 0)] + 1)
                                heads = (2 * y, 2 * y + 1) if i < 4 else (y,)
                                for n, h in enumerate(heads):
                                    s = slice(STRIP * h, STRIP * h + STRIP)
                                    off = lo + n * BANK
                                    for k0 in range(0, width, BANK):
                                        k1 = min(width, k0 + BANK)
                                        nc.tensor.matmul(ps[:, off + k0:off + k1], qa0[s, nxt, i * P:(i + 1) * P],
                                                         ka[s, nxt, k0:k1], start=True, stop=k1 < width)
                                for n, h in enumerate(heads):
                                    off = lo + n * BANK
                                    last = nc.tensor.matmul(ps[:, off + i * P:off + (i + 1) * P], identb[:, :],
                                                            maskb[:, 0, :], start=False, stop=True)
                                last.then_inc(du_full, 1)
                            elif kind == "MT":
                                pe.wait_ge(du_done, base + u if (b is not None or u) else 0)
                                for t in range(4):
                                    last = nc.tensor.transpose(ps[:, lo + t * P:lo + (t + 1) * P], mcat[:, 4 * x + t, :], ident)
                                last.then_inc(du_full, 1)
                            elif kind == "OT":
                                pe.wait_ge(ov_done, m0 + m_ot + 2)
                                for t in range(4):
                                    last = nc.tensor.transpose(ps[:, lo + t * P:lo + (t + 1) * P],
                                                               ot[:, m_ot % 2, t * P:(t + 1) * P], ident)
                                last.then_inc(du_full, 1)
                                m_ot += 1
                            elif kind == "ST":
                                par = g % 2
                                if y == 0 and x == 0:
                                    pe.wait_ge(du_done, base if g == 0 else base + at[(g - 1, "MT", 0, 0)] + 1)
                                if y == 0 and x == 1:
                                    pe.wait_ge(du_done, base + at[(g, "MT", 1, -1)] + 1)
                                c0 = max(BANK * x, P * y)
                                width = BANK * (x + 1) - c0
                                for h in range(G4):
                                    s = slice(STRIP * h, STRIP * h + STRIP)
                                    ub = 4 + e % 3
                                    pe.wait_ge(eu_done, e0 + e + 1)
                                    diagonal = c0 == P * y
                                    last = nc.tensor.matmul(bank(ub, width), ka[s, par, y * P:(y + 1) * P],
                                                            qa1[s, par, c0:c0 + width], start=True, stop=not diagonal)
                                    if diagonal:
                                        last = nc.tensor.matmul(bank(ub, P), identb[:, :], maskb[:, 1, :], start=False, stop=True)
                                    last.then_inc(eu_full, 1)
                                    e += 1
                            elif kind == "PV":
                                par = g % 2
                                c0 = max(BANK * x, P * y)
                                width = BANK * (x + 1) - c0
                                pe.wait_ge(eu_done, e0 + 4 * (q + 1) + 3)
                                if y == 0:
                                    pe.wait_ge(ov_done, m0 + m + 1)
                                final = y == 4 * x + 3
                                for h in range(G4):
                                    last = nc.tensor.matmul(
                                        ps[STRIP * h:STRIP * (h + 1), 7 * BANK + c0 - BANK * x:7 * BANK + c0 - BANK * x + width],
                                        va[:, par, y, h, :], pt[:, (4 * q + h) % 8, 0:width], start=y == 0, stop=final)
                                last.then_inc(pv_done, 1)
                                q += 1
                                m += final

                    passes(pe, walk)

                @block.scalar
                def _(act):
                    act.sem_inc(eu_done, 3)
                    act.sem_inc(ov_done, 1)
                    rounds_per_b = 2 * NG

                    def walk(sched, base, u0, b):
                        e0, q0, m0 = counts(b)
                        e = m = 0
                        for g, kind, x, y, u in sched:
                            if kind in ("Q", "K"):
                                c = "QK".index(kind)
                                act.wait_ge(du_full, base + u + 1)
                                src = ps[:, unit(u0, u) * 2 * BANK:(unit(u0, u) + 1) * 2 * BANK]
                                if kind == "Q":
                                    nc.scalar.activation(rnd[:, 0, :], src, ACT.Copy).then_inc(rounded, 1)
                                else:
                                    nc.scalar.activation(rnd[:, 1, :], src, ACT.Identity, bias=bias_k).then_inc(rounded, 1)
                            elif kind == "ST":
                                c0 = max(BANK * x, P * y)
                                width = BANK * (x + 1) - c0
                                act.wait_ge(pv_done, q0 + e // 4 + 1)
                                for h in range(G4):
                                    act.wait_ge(eu_full, e0 + e + 1)
                                    nc.scalar.activation(pt[:, e % 8, 0:width], bank(4 + e % 3, width), ACT.Exp,
                                                         scale=SCALE).then_inc(eu_done, 1)
                                    e += 1
                            elif kind == "PV" and y == 4 * x + 3:
                                act.wait_ge(pv_done, q0 + 2 + q_after[(g, x)])
                                nc.scalar.activation(ot[:, m % 2, :], bank(7), ACT.Copy).then_inc(ov_done, 1)
                                m += 1

                    q_after = {(g, half): 12 * g + (4 if half == 0 else 12) for g in range(NG) for half in range(2)}
                    passes(act, walk)

                @block.vector
                def _(dve):
                    nc.vector.memset(mcat[:, :, :], 0.0)
                    nc.vector.memset(va[:, :, :, :, :], 0.0)
                    dve.drain()
                    nc.vector.memset(va[:, :, :, :, HD:HD + 1], 1.0)
                    dve.drain()

                    def walk(sched, base, u0, b):
                        k0 = 0 if b is None else b * (2 * NG) + 2
                        k = m = 0
                        for g, kind, x, y, u in sched:
                            if u is None:
                                continue
                            nxt = (g + 1) % 2 if b is not None else 0
                            lo = unit(u0, u) * 2 * BANK
                            if kind in ("Q", "K"):
                                c = "QK".index(kind)
                                dve.wait_ge(rounded, k0 + k + 1)
                                k += 1
                                dst, coef = (qa0, coef_q) if kind == "Q" else (ka, coef_k)
                                nc.vector.scalar_tensor_tensor(dst[:, nxt, :], rnd[:, c, :], coef, ps[:, lo:lo + 2 * BANK],
                                                               ALU.mult, ALU.add).then_inc(du_done, 1)
                                continue
                            dve.wait_ge(du_full, base + u + 1)
                            if kind == "V":
                                nc.vector.tensor_copy(va[:, nxt, :, :, 0:HD],
                                                      ps[:, lo:lo + TB * STRIP].rearrange("p (t h c) -> p t h c", t=TB, h=G4))\
                                    .then_inc(du_done, 1)
                            elif kind == "S" and x < 4:
                                nc.vector.tensor_reduce(
                                    mcat[:, x, :].rearrange("p (h c) -> p h c", h=G4)[:, 2 * y:2 * y + 2, ONE_ROW],
                                    ps[:, lo:lo + 2 * BANK].rearrange("p (a k) -> p a k", a=2)[:, :, 0:(x + 1) * P],
                                    AX.X, ALU.max, negate=True).then_inc(du_done, 1)
                            elif kind == "S":
                                col = STRIP * y + ONE_ROW
                                nc.vector.tensor_reduce(mcat[:, x, col:col + 1], ps[:, lo:lo + (x + 1) * P],
                                                        AX.X, ALU.max, negate=True).then_inc(du_done, 1)
                            elif kind == "MT":
                                par = nxt if y == 0 else (g % 2)
                                half = slice(x * BANK, (x + 1) * BANK)
                                nc.vector.tensor_tensor(qa1[:, par, half], ps[:, lo:lo + BANK], qa0[:, par, half], ALU.add)\
                                    .then_inc(du_done, 1)
                            elif kind == "OT":
                                half, go = x, g if y == 0 else g - 1
                                turned = ps[:, lo:lo + BANK].rearrange("p (t h c) -> p t h c", t=4, h=G4)
                                nc.vector.reciprocal(rs[:, half, :, :], turned[:, :, :, HD])
                                dve.drain()
                                dst = o[:, bass.ds(b * TB + 4 * half, 4), go * 32:go * 32 + 32]
                                nc.vector.tensor_tensor(
                                    dst.rearrange("p t (h c) -> p t h c", h=G4), turned[:, :, :, 0:HD],
                                    rs[:, half, :, :].rearrange("p t (h a) -> p t h a", a=1).to_broadcast([P, 4, G4, HD]),
                                    ALU.mult).then_inc(du_done, 1)

                    passes(dve, walk)

                @block.gpsimd
                def _(pool):
                    nc.gpsimd.tensor_copy(xt[:, :], ft[:, 0:N]).then_inc(xt_ready, 1)
                    used = {g: u for g, kind, x, y, u in BODY if kind == "V"}[NG - 2]
                    with pool.Fori(0, B - 1) as b:
                        pool.wait_ge(du_full, b * BODY_USES + PRO + used + 1)
                        nc.gpsimd.tensor_copy(xt[:, :], ft[:, bass.ds(b * N + N, N)]).then_inc(xt_ready, 1)


        def scope(fn):
            def run(tag):
                with ExitStack() as mine:
                    def own(name, shape, dt=F32):
                        return mine.enter_context(nc.sbuf_tensor(f"{tag}_{fn.__name__}_{name}", shape, dt))
                    fn(tag, own, lambda name: sem(f"{tag}_{fn.__name__}_{name}"))
            return run

        @scope
        def first_norm(tag, own, sem):
            xs = own("xs", [P, 2, 4, D])
            var, dev, norm, turned, out_, copied = map(sem, ("var", "dev", "norm", "turned", "evacuated", "copied"))
            with nc.Block() as block:
                @block.vector
                def _(dve):
                    credit(dve, norm)
                    if tag == "f1":
                        dve.wait_ge(s_x, 16 * B)

                    def body(n0):
                        for par in range(2):
                            n = n0 + par
                            stats(dve, lambda t: tile(x, n, t), par).then_inc(var, 1)
                        for par in range(2):
                            n = n0 + par
                            dve.wait_ge(dev, n + 1)
                            before(dve, turned, n)
                            before(dve, copied, n)
                            normalise(dve, par, lambda t: xs[:, par, t, :], lambda t: tile(x, n, t)).then_inc(norm, 1)
                    quads(dve, body)

                @block.scalar
                def _(act):
                    credit(act, out_)

                    def body(n0):
                        for par in range(2):
                            act.wait_ge(var, n0 + par + 1)
                            nc.scalar.activation(sd[:, par, :], ve[:, par, :], ACT.Sqrt).then_inc(dev, 1)
                        for par in range(2):
                            now(act, turned, n0 + par)
                            nc.scalar.activation(ft[:, bass.ds((n0 + par) * BANK, BANK)], bank(par), ACT.Copy).then_inc(out_, 1)
                    quads(act, body)

                @block.tensor
                def _(pe):
                    credit(pe, turned)

                    def body(n0):
                        for par in range(2):
                            now(pe, norm, n0 + par)
                            before(pe, out_, n0 + par)
                            turn(par, lambda t: xs[:, par, t, :]).then_inc(turned, 1)
                    quads(pe, body)

                @block.gpsimd
                def _(pool):
                    credit(pool, copied)

                    def body(n0):
                        for par in range(2):
                            now(pool, norm, n0 + par)
                            nc.gpsimd.tensor_copy(tiles(xn, n0 + par), xs[:, par, :, :]).then_inc(copied, 1)
                    quads(pool, body)

        @scope
        def after_attention(tag, own, sem):
            mid = tag == "mid"
            os_, ots = own("o", [P, 2, 4, D]), own("ot", [P, 2, BANK])
            ys, zs, hs = own("y", [P, 2, 4, D]), own("z", [P, 2, 4, D]), own("h", [P, 2, 4, D])
            hts = own("ht", [P, 2, BANK])
            (staged, turned, ot_ready, product, summed, var, dev, norm, turned2, ht_ready, kept, scored, noted,
             gained, entered) = map(sem, ("staged", "turned", "ot_ready", "product", "summed", "var", "dev", "norm",
                                          "turned2", "ht_ready", "kept", "scored", "noted", "gained", "entered"))
            w_out = wo_s if mid else w_o_s
            gain, shift = (mcols[:, 2:3], mcols[:, 3:4]) if mid else (fcols[:, E * FC:E * FC + 1], fcols[:, E * FC + 1:E * FC + 2])

            with nc.Block() as block:
                @block.gpsimd
                def _(pool):
                    credit(pool, staged, kept, gained, entered)

                    def body(n0):
                        for par in range(2):
                            before(pool, turned, n0 + par)
                            nc.gpsimd.tensor_copy(os_[:, par, :, :], tiles(o, n0 + par)).then_inc(staged, 1)
                        if not mid:
                            for par in range(2):
                                n = n0 + par
                                now(pool, norm, n)
                                now(pool, staged, n)
                                before(pool, entered, n)
                                nc.gpsimd.tensor_tensor(hs[:, par, :, :], zs[:, par, :, :], wide(rows[:, 0, :]), ALU.mult).then_inc(gained, 1)
                                pool.drain()
                                nc.gpsimd.tensor_tensor(hs[:, par, :, :], hs[:, par, :, :], wide(rows[:, 1, :]), ALU.add)
                                pool.drain()
                                nc.gpsimd.tensor_copy(tiles(o, n), hs[:, par, :, :]).then_inc(entered, 1)
                        for par in range(2):
                            n = n0 + par
                            now(pool, ht_ready, n)
                            nc.gpsimd.tensor_copy(ft[:, bass.ds(n * BANK, BANK)], hts[:, par, :]).then_inc(kept, 1)
                    quads(pool, body)

                @block.tensor
                def _(pe):
                    credit(pe, turned, product, turned2, scored)

                    def body(n0):
                        for par in range(2):
                            now(pe, staged, n0 + par)
                            before(pe, ot_ready, n0 + par)
                            turn(par, lambda t: os_[:, par, t, :]).then_inc(turned, 1)
                        for par in range(2):
                            now(pe, ot_ready, n0 + par)
                            before(pe, summed, n0 + par)
                            for t in range(4):
                                last = nc.tensor.matmul(ps[:, (2 + par) * BANK + t * P:(2 + par) * BANK + (t + 1) * P],
                                                        ots[:, par, t * P:(t + 1) * P], w_out[:, :], start=True, stop=True)
                            last.then_inc(product, 1)
                        for par in range(2):
                            now(pe, norm, n0 + par)
                            before(pe, ht_ready, n0 + par)
                            turn(4 + par, lambda t: zs[:, par, t, :]).then_inc(turned2, 1)
                        if not mid:
                            for par in range(2):
                                now(pe, ht_ready, n0 + par)
                                before(pe, noted, n0 + par)
                                for t in range(4):
                                    last = nc.tensor.matmul(ps[:, (6 + par) * BANK + t * E:(6 + par) * BANK + (t + 1) * E],
                                                            hts[:, par, t * P:(t + 1) * P], wg_s[:, :], start=True, stop=True)
                                last.then_inc(scored, 1)
                    quads(pe, body)

                @block.scalar
                def _(act):
                    credit(act, ot_ready, ht_ready)

                    def body(n0):
                        for par in range(2):
                            now(act, turned, n0 + par)
                            before(act, product, n0 + par)
                            nc.scalar.activation(ots[:, par, :], bank(par), ACT.Copy).then_inc(ot_ready, 1)
                        for par in range(2):
                            act.wait_ge(var, n0 + par + 1)
                            nc.scalar.activation(sd[:, par, :], ve[:, par, :], ACT.Sqrt).then_inc(dev, 1)
                        for par in range(2):
                            now(act, turned2, n0 + par)
                            before(act, kept, n0 + par)
                            if not mid:
                                before(act, scored, n0 + par)
                            nc.scalar.activation(hts[:, par, :], bank(4 + par), ACT.Identity, bias=shift, scale=gain).then_inc(ht_ready, 1)
                    quads(act, body)

                @block.vector
                def _(dve):
                    credit(dve, summed, norm, noted)

                    def body(n0):
                        for par in range(2):
                            n = n0 + par
                            now(dve, product, n)
                            y = (lambda t: tile(xn, n, t)) if mid else (lambda t: ys[:, par, t, :])
                            y4 = tiles(xn, n) if mid else ys[:, par, :, :]
                            nc.vector.tensor_tensor(y4, tiles(xn, n), quad(2 + par), ALU.add).then_inc(summed, 1)
                            now(dve, summed, n)
                            if mid:
                                nc.vector.tensor_tensor(y4, y4, wide(mrows[:, 3 * D:4 * D]), ALU.add)
                                dve.drain()
                            stats(dve, y, par).then_inc(var, 1)
                        for par in range(2):
                            n = n0 + par
                            y = (lambda t: tile(xn, n, t)) if mid else (lambda t: ys[:, par, t, :])
                            dve.wait_ge(dev, n + 1)
                            before(dve, turned2, n)
                            if not mid:
                                before(dve, gained, n)
                            normalise(dve, par, lambda t: zs[:, par, t, :], y).then_inc(norm, 1)
                        if not mid:
                            for par in range(2):
                                n = n0 + par
                                now(dve, scored, n)
                                nc.vector.tensor_copy(tiles(wr, n), bank(6 + par, 4 * E).rearrange("p (a e) -> p a e", a=4)).then_inc(noted, 1)
                    quads(dve, body)

        @scope
        def route(tag, own, sem):
            ex, top, rest = own("exp", [P, NT, E]), own("top", [P, NT, 8]), own("rest", [P, NT, E])
            peak, total = own("peak", [P, NT]), own("total", [P, NT])
            wt = own("wt", [E, NT * P])
            centred, expd, shares, turned, wt_ready, biased = map(sem, ("centred", "exp", "shares", "turned", "wt_ready", "biased"))

            def bc(ap):
                return ap.rearrange("p (t a) -> p t a", a=1).to_broadcast([P, NT, E])

            with nc.Block() as block:
                @block.vector
                def _(dve):
                    nc.vector.tensor_reduce(peak[:, :], wr[:, :, :], AX.X, ALU.max)
                    dve.drain()
                    nc.vector.tensor_tensor(ex[:, :, :], wr[:, :, :], bc(peak[:, :]), ALU.subtract).then_inc(centred, 1)
                    dve.wait_ge(expd, 1)
                    for t in range(NT):
                        nc.vector.max(top[:, t, :], ex[:, t, :])
                    dve.drain()
                    nc.vector.memset(top[:, :, 2:8], -1.0)
                    nc.vector.tensor_tensor(total[:, :], top[:, :, 0], top[:, :, 1], ALU.add)
                    dve.drain()
                    for t in range(NT):
                        nc.vector.match_replace(rest[:, t, :], top[:, t, :], ex[:, t, :], 0.0)
                    nc.vector.reciprocal(peak[:, :], total[:, :])
                    dve.drain()
                    nc.vector.tensor_tensor(ex[:, :, :], ex[:, :, :], rest[:, :, :], ALU.subtract)
                    dve.drain()
                    nc.vector.tensor_tensor(wr[:, :, :], ex[:, :, :], bc(peak[:, :]), ALU.mult).then_inc(shares, 1)
                    for n in range(QUAD):
                        dve.wait_ge(turned, n + 1)
                        nc.vector.tensor_copy(wt[:, n * BANK:(n + 1) * BANK], ps[0:E, (n % 4) * BANK:(n % 4 + 1) * BANK]).then_inc(wt_ready, 1)
                    for n in range(QUAD):
                        dve.wait_ge(turned, QUAD + n + 1)
                        nc.vector.tensor_tensor(o[:, 4 * n:4 * n + 4, :], o[:, 4 * n:4 * n + 4, :], quad(4 + n % 4), ALU.add).then_inc(biased, 1)

                @block.scalar
                def _(act):
                    act.wait_ge(centred, 1)
                    nc.scalar.activation(ex[:, :, :], ex[:, :, :], ACT.Exp).then_inc(expd, 1)

                @block.tensor
                def _(pe):
                    pe.wait_ge(shares, 1)
                    for n in range(QUAD):
                        if n >= 4:
                            pe.wait_ge(wt_ready, n - 3)
                        for t in range(4):
                            last = nc.tensor.transpose(ps[0:E, (n % 4) * BANK + t * P:(n % 4) * BANK + (t + 1) * P],
                                                       wr[:, 4 * n + t, :], ident)
                        last.then_inc(turned, 1)
                    if tag == "f1":
                        pe.wait_ge(s_big, 16 * BIG_LOADS)
                    for n in range(QUAD):
                        pe.wait_ge(wt_ready, n + 1)
                        if n >= 4:
                            pe.wait_ge(biased, n - 3)
                        for t in range(4):
                            last = nc.tensor.matmul(ps[:, (4 + n % 4) * BANK + t * P:(4 + n % 4) * BANK + (t + 1) * P],
                                                    wt[:, n * BANK + t * P:n * BANK + (t + 1) * P], bb2s[:, :], start=True, stop=True)
                        last.then_inc(turned, 1)

        @scope
        def experts(tag, own, sem):
            acc, ws = own("acc", [P, 2, 4, D]), own("shares", [P, 2, 4, E])
            h1 = own("h1", [P, 2, FC, BANK])
            zs, hs, fs = own("z", [P, 2, 4, D]), own("h", [P, 2, 4, D]), own("f", [P, 2, 4, D])
            (staged, up, gelu, down, summed, var, dev, norm, gained, shifted, added) = map(sem, (
                "staged", "up", "gelu", "down", "summed", "var", "dev", "norm", "gained", "shifted", "added"))
            with nc.Block() as block:
                @block.gpsimd
                def _(pool):
                    credit(pool, staged, gained, shifted)

                    def body(n0):
                        for par in range(2):
                            n = n0 + par
                            before(pool, norm, n)
                            nc.gpsimd.tensor_copy(ws[:, par, :, :], tiles(wr, n))
                            nc.gpsimd.tensor_copy(acc[:, par, :, :], tiles(o, n)).then_inc(staged, 1)
                        for par in range(2):
                            n = n0 + par
                            now(pool, norm, n)
                            before(pool, shifted, n)
                            nc.gpsimd.tensor_tensor(hs[:, par, :, :], zs[:, par, :, :], wide(rows[:, 2, :]), ALU.mult).then_inc(gained, 1)
                            now(pool, gained, n)
                            before(pool, added, n)
                            nc.gpsimd.tensor_tensor(fs[:, par, :, :], hs[:, par, :, :], wide(rows[:, 3, :]), ALU.add).then_inc(shifted, 1)
                    quads(pool, body)

                @block.tensor
                def _(pe):
                    def body(n0):
                        for par in range(2):
                            n = n0 + par
                            for e in range(E + 1):
                                if e < E:
                                    for c in range(FC):
                                        u = (n * E + e) * FC + c
                                        pe.wait_ge(gelu, u + 1)
                                        nc.tensor.matmul(bank(c), w1s[:, e, c * P:(c + 1) * P], ft[:, bass.ds(n * BANK, BANK)],
                                                         start=True, stop=True).then_inc(up, 1)
                                if e:
                                    k = n * E + e - 1
                                    pe.wait_ge(gelu, (k + 1) * FC + 4)
                                    before(pe, summed, k)
                                    for t in range(4):
                                        for c in range(FC):
                                            col = (4 + (e - 1) % 2) * BANK + t * P
                                            last = nc.tensor.matmul(ps[:, col:col + P], h1[:, (e - 1) % 2, c, t * P:(t + 1) * P],
                                                                    w2s[:, e - 1, c, :], start=c == 0, stop=c == FC - 1)
                                    last.then_inc(down, 1)
                    credit(pe, down)
                    quads(pe, body)

                @block.scalar
                def _(act):
                    act.sem_inc(gelu, 4)

                    def body(n0):
                        for par in range(2):
                            n = n0 + par
                            for e in range(E):
                                before(act, down, n * E + e)
                                for c in range(FC):
                                    act.wait_ge(up, (n * E + e) * FC + c + 1)
                                    nc.scalar.activation(h1[:, e % 2, c, :], bank(c), ACT.Gelu_apprx_tanh,
                                                         bias=fcols[:, e * FC + c:e * FC + c + 1]).then_inc(gelu, 1)
                            act.wait_ge(var, n + 1)
                            nc.scalar.activation(sd[:, par, :], ve[:, par, :], ACT.Sqrt).then_inc(dev, 1)
                    quads(act, body)

                @block.vector
                def _(dve):
                    credit(dve, summed, norm, added)

                    def body(n0):
                        for par in range(2):
                            n = n0 + par
                            now(dve, staged, n)
                            for e in range(E):
                                now(dve, down, n * E + e)
                                for t in range(4):
                                    last = nc.vector.scalar_tensor_tensor(
                                        acc[:, par, t, :], ps[:, (4 + e % 2) * BANK + t * P:(4 + e % 2) * BANK + (t + 1) * P],
                                        ws[:, par, t, e:e + 1], acc[:, par, t, :], ALU.mult, ALU.add)
                                last.then_inc(summed, 1)
                                now(dve, summed, n * E + e)
                            stats(dve, lambda t: acc[:, par, t, :], par).then_inc(var, 1)
                            dve.wait_ge(dev, n + 1)
                            before(dve, gained, n)
                            normalise(dve, par, lambda t: zs[:, par, t, :], lambda t: acc[:, par, t, :]).then_inc(norm, 1)
                        for par in range(2):
                            n = n0 + par
                            now(dve, shifted, n)
                            nc.vector.tensor_tensor(tiles(x, n), tiles(x, n), fs[:, par, :, :], ALU.add).then_inc(added, 1)
                    quads(dve, body)

        @scope
        def project(tag, own, sem):
            xs, zs, zt = own("xs", [P, 2, 4, D]), own("z", [P, 2, 4, D]), own("zt", [P, 2, BANK])
            var, dev, kept, norm, twice, turned, zt_ready, product, out_ = map(sem, (
                "var", "dev", "kept", "norm", "twice", "turned", "zt_ready", "product", "out"))
            qkv = buffers["qkv"]
            with nc.Block() as block:
                @block.vector
                def _(dve):
                    credit(dve, norm, twice)
                    dve.sem_inc(out_, 4)

                    def body(n0):
                        for par in range(2):
                            stats(dve, lambda t: tile(x, n0 + par, t), par).then_inc(var, 1)
                        for par in range(2):
                            n = n0 + par
                            dve.wait_ge(dev, n0 * 2 + par + 1)
                            before(dve, kept, n)
                            normalise(dve, par, lambda t: xs[:, par, t, :], lambda t: tile(x, n, t)).then_inc(norm, 1)
                            now(dve, norm, n)
                            stats(dve, lambda t: xs[:, par, t, :], par).then_inc(var, 1)
                        for par in range(2):
                            n = n0 + par
                            dve.wait_ge(dev, n0 * 2 + 2 + par + 1)
                            before(dve, turned, n)
                            normalise(dve, par, lambda t: zs[:, par, t, :], lambda t: xs[:, par, t, :]).then_inc(twice, 1)
                        for par in range(2):
                            n = n0 + par
                            for t in range(4):
                                dve.wait_ge(product, n * 4 + t + 9)
                                nc.vector.tensor_tensor(tile(qkv, n, t), bank(2 + t, 3 * D), mrows[:, 0:3 * D], ALU.add).then_inc(out_, 1)
                    quads(dve, body)

                @block.scalar
                def _(act):
                    credit(act, zt_ready)

                    def body(n0):
                        for k in range(4):
                            act.wait_ge(var, n0 * 2 + k + 1)
                            nc.scalar.activation(sd[:, k % 2, :], ve[:, k % 2, :], ACT.Sqrt).then_inc(dev, 1)
                        for par in range(2):
                            n = n0 + par
                            now(act, turned, n)
                            act.wait_ge(product, n * 4 + 4)
                            nc.scalar.activation(zt[:, par, :], bank(par), ACT.Identity, bias=mcols[:, 1:2], scale=mcols[:, 0:1]).then_inc(zt_ready, 1)
                    quads(act, body)

                @block.tensor
                def _(pe):
                    credit(pe, turned)
                    pe.sem_inc(product, 8)

                    def body(n0):
                        for par in range(2):
                            now(pe, twice, n0 + par)
                            before(pe, zt_ready, n0 + par)
                            turn(par, lambda t: zs[:, par, t, :]).then_inc(turned, 1)
                        for par in range(2):
                            n = n0 + par
                            now(pe, zt_ready, n)
                            for t in range(4):
                                pe.wait_ge(out_, n * 4 + t + 1)
                                nc.tensor.matmul(bank(2 + t, 3 * D), zt[:, par, t * P:(t + 1) * P], wall[:, :],
                                                 start=True, stop=True).then_inc(product, 1)
                    quads(pe, body)

                @block.gpsimd
                def _(pool):
                    credit(pool, kept)

                    def body(n0):
                        for par in range(2):
                            now(pool, norm, n0 + par)
                            nc.gpsimd.tensor_copy(tiles(xn, n0 + par), xs[:, par, :, :]).then_inc(kept, 1)
                    quads(pool, body)

        @scope
        def linear_attention(tag, own, sem):
            VW = HD + 1
            low, expo, feat = (own(n, [P, 2, 2 * D]) for n in ("low", "exp", "feat"))
            vx = own("vx", [P, 2, H, VW])
            pr1, pr2 = own("pr1", [P, 2, H, HD, VW]), own("pr2", [P, 2, H, VW, HD])
            kv, res = own("kv", [P, 2, HD, VW]), own("res", [P, 2, H, VW])
            den = own("den", [P, 2, H])
            lowered, expd, featured, copied, outer, summed, weighed, done = map(sem, (
                "lowered", "exp", "featured", "copied", "outer", "summed", "weighed", "done"))
            qkv = buffers["qkv"]

            def pairs(eng, body):
                with eng.Fori(0, NT // 2) as i:
                    for par in range(2):
                        body(i * 2 + par, par)

            def one(t, n, a, b):
                return t[:, bass.ds(n, 1), a:b].rearrange("p a d -> p (a d)")

            with nc.Block() as block:
                @block.vector
                def _(dve):
                    credit(dve, lowered, featured, summed, done)

                    def features(n, par):
                        before(dve, weighed, n)
                        nc.vector.tensor_scalar(low[:, par, :], one(qkv, n, 0, 2 * D), 0.0, None, ALU.min).then_inc(lowered, 1)
                        dve.wait_ge(expd, n + 1)
                        nc.vector.scalar_tensor_tensor(feat[:, par, :], one(qkv, n, 0, 2 * D), 0.0, expo[:, par, :], ALU.max, ALU.add).then_inc(featured, 1)

                    def rest(n, par):
                        dve.wait_ge(outer, n + 1)
                        nc.vector.tensor_reduce(kv[:, par, :, :].rearrange("p d e -> p (d e)"),
                                                pr1[:, par, :, :, :].rearrange("p h d e -> p (d e) h"), AX.X, ALU.add).then_inc(summed, 1)
                        now(dve, summed, n)
                        fq = feat[:, par, 0:D].rearrange("p (h a d) -> p h a d", a=1, d=HD)
                        kvt = kv[:, par, :, :].rearrange("p (a d) e -> p a e d", a=1)
                        nc.vector.tensor_tensor(pr2[:, par, :, :, :], fq.to_broadcast([P, H, VW, HD]), kvt.to_broadcast([P, H, VW, HD]),
                                                ALU.mult).then_inc(weighed, 1)
                        now(dve, weighed, n)
                        nc.vector.tensor_reduce(res[:, par, :, :], pr2[:, par, :, :, :], AX.X, ALU.add)
                        dve.drain()
                        nc.vector.tensor_scalar(den[:, par, :], res[:, par, :, HD], 1e-6, None, ALU.add)
                        dve.drain()
                        nc.vector.reciprocal(den[:, par, :], den[:, par, :])
                        dve.drain()
                        nc.vector.tensor_tensor(one(o, n, 0, D).rearrange("p (h e) -> p h e", h=H), res[:, par, :, 0:HD],
                                                den[:, par, :].rearrange("p (h a) -> p h a", a=1).to_broadcast([P, H, HD]),
                                                ALU.mult).then_inc(done, 1)

                    credit(dve, weighed)
                    with dve.Fori(0, NT // 2) as i:
                        features(i * 2, 0)
                        features(i * 2 + 1, 1)
                        rest(i * 2, 0)
                        rest(i * 2 + 1, 1)

                @block.scalar
                def _(act):
                    def body(n, par):
                        now(act, lowered, n)
                        before(act, featured, n)
                        nc.scalar.activation(expo[:, par, :], low[:, par, :], ACT.Exp).then_inc(expd, 1)
                    pairs(act, body)

                @block.gpsimd
                def _(pool):
                    nc.gpsimd.memset(vx[:, :, :, HD:VW], 1.0).then_inc(copied, 1)
                    pool.wait_ge(copied, 1)

                    def body(n, par):
                        nc.gpsimd.tensor_copy(vx[:, par, :, 0:HD], one(qkv, n, 2 * D, 3 * D).rearrange("p (h e) -> p h e", h=H)).then_inc(copied, 1)
                        pool.wait_ge(copied, n + 2)
                        now(pool, featured, n)
                        before(pool, summed, n)
                        fk = feat[:, par, D:2 * D].rearrange("p (h d a) -> p h d a", h=H, a=1)
                        v = vx[:, par, :, :].rearrange("p h (a e) -> p h a e", a=1)
                        nc.gpsimd.tensor_tensor(pr1[:, par, :, :, :], fk.to_broadcast([P, H, HD, VW]), v.to_broadcast([P, H, HD, VW]),
                                                ALU.mult).then_inc(outer, 1)
                    pairs(pool, body)

        @scope
        def mlp(tag, own, sem):
            h1 = own("h1", [P, 2, FC, BANK])
            ys, us = own("y", [P, 2, 4, D]), own("u", [P, 2, 4, D])
            up, gelu, down, summed = map(sem, ("up", "gelu", "down", "summed"))
            with nc.Block() as block:
                @block.tensor
                def _(pe):
                    credit(pe, down)

                    def body(n0):
                        for par in range(2):
                            n = n0 + par
                            for c in range(FC):
                                pe.wait_ge(gelu, n * FC + c + 1)
                                nc.tensor.matmul(bank(c), fc_s[:, c * P:(c + 1) * P], ft[:, bass.ds(n * BANK, BANK)],
                                                 start=True, stop=True).then_inc(up, 1)
                        for par in range(2):
                            n = n0 + par
                            pe.wait_ge(gelu, (n + 1) * FC + 4)
                            before(pe, summed, n)
                            for t in range(4):
                                for c in range(FC):
                                    last = nc.tensor.matmul(ps[:, (4 + par) * BANK + t * P:(4 + par) * BANK + (t + 1) * P],
                                                            h1[:, par, c, t * P:(t + 1) * P], pj_s[:, c, :],
                                                            start=c == 0, stop=c == FC - 1)
                            last.then_inc(down, 1)
                    quads(pe, body)

                @block.scalar
                def _(act):
                    act.sem_inc(gelu, 4)

                    def body(n0):
                        for par in range(2):
                            n = n0 + par
                            before(act, down, n)
                            for c in range(FC):
                                act.wait_ge(up, n * FC + c + 1)
                                nc.scalar.activation(h1[:, par, c, :], bank(c), ACT.Gelu, bias=mcols[:, 4 + c:5 + c]).then_inc(gelu, 1)
                    quads(act, body)

                @block.vector
                def _(dve):
                    credit(dve, summed)

                    def body(n0):
                        for par in range(2):
                            n = n0 + par
                            now(dve, down, n)
                            nc.vector.tensor_tensor(ys[:, par, :, :], tiles(xn, n), quad(4 + par), ALU.add).then_inc(summed, 1)
                            now(dve, summed, n)
                            nc.vector.tensor_tensor(us[:, par, :, :], ys[:, par, :, :], wide(mrows[:, 4 * D:5 * D]), ALU.add)
                            dve.drain()
                            nc.vector.tensor_tensor(tiles(x, n), tiles(x, n), us[:, par, :, :], ALU.add)
                        dve.drain()
                    quads(dve, body)

        def linear_layer(tag):
            with ExitStack() as mine:
                buffers["qkv"] = mine.enter_context(nc.sbuf_tensor(f"{tag}_qkv", [P, NT, 3 * D], F32))
                project(tag)
                linear_attention(tag)
            after_attention(tag)
            mlp(tag)

        buffers = {}
        ffn("f1")
        linear_layer("mid")
        ffn("f2")
        s_out = sem("out_stored")
        with nc.Block() as block:
            @block.sync
            def _(sp):
                sp.dma_start(out.rearrange("b (t p) d -> p (b t) d", p=P), x[:, :, :]).then_inc(s_out, 16)
                sp.wait_ge(s_out, 16)


def constants():
    i = np.arange(P)
    row = i % STRIP
    c = np.zeros((P, 3 * P + 4), np.float32)
    c[:, 0:P] = np.eye(P)
    c[:, P:2 * P] = np.where(i[None, :] > i[:, None], NEG, 0)
    c[:, 2 * P:3 * P] = np.where(i[:, None] > i[None, :], NEG, 0)
    c[:, 3 * P] = np.where((row >= 2 * HD) & (row < 3 * HD), -1, 0) + (row == ONE_ROW)
    c[:, 3 * P + 1] = np.where((row >= HD) & (row < 2 * HD), -1, 0)
    c[:, 3 * P + 2] = row == ONE_ROW
    return c


_INS = ['L0_attn_q_x', 'L0_attn_ln1_w', 'L0_attn_ln1_b', 'L0_attn_wq', 'L0_attn_bq', 'L0_attn_wk', 'L0_attn_bk',
        'L0_attn_wv', 'L0_attn_bv', 'L0_attn_wo', 'L0_attn_bo', 'L0_attn_ln2_w', 'L0_attn_ln2_b', 'L0_attn_fc_w',
        'L0_attn_fc_b', 'L0_attn_proj_w', 'L0_attn_proj_b', 'L0_ffn_w_qkv', 'L0_ffn_w_o', 'L0_ffn_g1', 'L0_ffn_b1',
        'L0_ffn_wg', 'L0_ffn_w1', 'L0_ffn_bb1', 'L0_ffn_w2', 'L0_ffn_bb2', 'L0_ffn_g2', 'L0_ffn_b2']


def kernel(**inputs):
    import concourse.bacc as _bacc
    from concourse.bass_utils import run_bass_kernel_spmd as _run

    nc = _bacc.Bacc("TRN2", target_bir_lowering=False, num_devices=1)
    arrays, args = {}, []
    for name in _INS:
        a = np.ascontiguousarray(inputs[name])
        arrays[f"in_{name}"] = a
        args.append(nc.dram_tensor(f"in_{name}", a.shape, mybir.dt.from_np(a.dtype), kind="ExternalInput").ap())
    arrays["constants"] = constants()
    args.append(nc.dram_tensor("constants", arrays["constants"].shape, F32, kind="ExternalInput").ap())
    args.append(nc.dram_tensor("out_dram", (B, N, D), F32, kind="ExternalOutput").ap())
    program(nc, *args)
    r = _run(nc, [arrays], core_ids=[0])
    return r.results[0]["out_dram"]
```

```python
import math
from collections import namedtuple
from contextlib import ExitStack

import concourse.bass as bass
import numpy as np
from concourse import mybir
from concourse.alu_op_type import AluOpType as ALU

F32 = mybir.dt.float32
F32R = mybir.dt.float32r
BF16 = mybir.dt.bfloat16
ACT = mybir.ActivationFunctionType
AX = mybir.AxisListType

B, N, D, H = 4, 1024, 128, 16
HD = D // H
E, F = 8, 512
P = 128
TB = N // P
NT = B * TB
G4 = 4
NG = H // G4
STRIP = P // G4
FC = F // P
EPS = 1e-5
NEG = -1e30
SCALE = 1.0 / math.sqrt(HD)
BANK = 512
BIG_LOADS = 1 + 3 + 1 + 1 + 1 + 5
ONE_ROW = 3 * HD
QUAD = NT // 4


Item = namedtuple("Item", "step kind x y du eu")
UNIT_BANKS, EXP_BANKS, SUM_BANK = 2, 3, 7
SLOTS = 3


def spread(items, lo=0.0, hi=1.0):
    total, at, out = sum(t for *_, t in items) or 1, 0.0, []
    for kind, x, y, t in items:
        out.append((lo + (hi - lo) * at / total, (kind, x, y)))
        at += t
    return out


def scores(i, x):
    return BANK * x, min((i + 1) * P, BANK * (x + 1))


def maxima_uses():
    def use(i, x, pair):
        k0, k1 = scores(i, x)
        return ("S", (i, x), pair, 2 * (k1 - k0) / 0.96 + 65)
    low = [use(i, 0, pair) for i in range(4) for pair in range(2)]
    high = [use(i, x, pair) for i in range(4, TB) for x in range(2) for pair in range(2)]
    return low + high[:3] + [("MT", 0, 0, 620)] + high[3:]


def width_of(half, j):
    c0 = max(BANK * half, P * j)
    return c0, BANK * (half + 1) - c0


def current_uses():
    groups = [(0, j) for j in range(4)] + [(1, j) for j in range(TB)]
    out = []
    for n, (half, j) in enumerate(groups):
        for pair in range(2):
            out.append(("ST", (half, j), pair, 2 * (width_of(half, j)[1] / 1.2 + 52)))
        if n >= 2:
            out.append(("PV", *groups[n - 2], 0))
        if n == 7:
            out.append(("OT", 0, 0, 0))
    return out + [("PV", *groups[-2], 0), ("PV", *groups[-1], 0)]


def projections():
    return [("P", qk, c, 480) for qk in range(2) for c in range(2)] + [("V", half, 0, 200) for half in range(2)]


def numbered(steps):
    out, du, eu = [], 0, 0
    for g, items in steps:
        for _, (kind, x, y) in sorted(items, key=lambda it: it[0]):
            uses_unit, banks = kind in ("S", "MT", "OT"), {"ST": 2, "P": 1, "V": 1}.get(kind, 0)
            out.append(Item(g, kind, x, y, du if uses_unit else None, eu if banks else None))
            du += uses_unit
            eu += banks
    return out, du, eu


def batch_element(last):
    steps = []
    for g in range(NG):
        items = spread(current_uses())
        units = [("MT", 1, 0, 620)]
        if not (last and g == NG - 1):
            units += maxima_uses()
        items += spread(units)
        if g:
            items.append((0.07, ("OT", 1, -1)))
        if not (last and g == NG - 1):
            items.append((-1.0, ("L", 1, 0)))
        if not (last and g >= NG - 2):
            items.append((0.8, ("L", 0, 0)))
        if not (last and g >= NG - 2):
            items += spread(projections(), 0.15, 0.75)
        if g == NG - 1:
            items.append((2.0, ("OT", 1, 0)))
        steps.append((g, items))
    return numbered(steps)


PROLOGUE, PRO_UNITS, PRO_EXPS = numbered([
    (-2, spread(projections()) + [(2.0, ("Z", 0, 0))]),
    (-1, spread(projections(), 0, 0.3) + [(0.34, ("L", 0, 0))] + spread(maxima_uses(), 0.35, 1.0))])
BODY, BODY_UNITS, BODY_EXPS = batch_element(False)
LAST_BODY = batch_element(True)[0]
assert BODY_UNITS % 2 == 0 and BODY_EXPS % EXP_BANKS == 0 and PRO_EXPS % EXP_BANKS == 0
QUEUE = [(0, j) for j in range(4)] + [(1, j) for j in range(TB)]
GROUPS_PV = len(QUEUE) * NG
assert 12 % SLOTS == 0


def program(nc, q_x, ln1_w, ln1_b, wq, bq, wk, bk, wv, bv, wo, bo, ln2_w, ln2_b, fc_w, fc_b, proj_w, proj_b,
            w_qkv, w_o, g1, b1, wg, w1, bb1, w2, bb2, g2, b2, consts, out):
    with ExitStack() as ctx:
        def sb(name, shape, dt=F32):
            return ctx.enter_context(nc.sbuf_tensor("sb_" + name, shape, dt))

        def sem(name):
            return ctx.enter_context(nc.semaphore(name))

        x = sb("x", [P, NT, D])
        xn = sb("xn", [P, NT, D])
        o = sb("o", [P, NT, D])
        ft = sb("ft", [P, NT * P])
        wr = sb("wr", [P, NT, E])

        cst = sb("cst", [P, 2 * P + 4])
        ident = cst[:, 0:P]
        coef_k, coef_q, one_row, one = (cst[:, 2 * P + i:2 * P + i + 1] for i in range(4))
        gate = sb("gate", [P, 1])
        identb = sb("identb", [P, P], BF16)
        maskb = sb("maskb", [P, P], BF16)

        wqkv = sb("wqkv", [P, 3 * D])
        wqk = sb("wqk", [P, NG, 2, P])
        w_o_s = sb("w_o_s", [P, D])
        wg_s = sb("wg_s", [P, E])
        by_feature = sb("by_feature", [E * FC + 2, P])
        fcols = sb("fcols", [P, E * FC + 2])
        bb2s = sb("bb2s", [E, D])
        rows = sb("rows", [P, 4, D])

        wall = sb("wall", [P, 3 * D])
        wo_s = sb("wo_s", [P, D])
        fc_s = sb("fc_s", [P, F])
        pj_s = sb("pj_s", [P, FC, D])
        by_feature2 = sb("by_feature2", [4 + FC, P])
        mcols = sb("mcols", [P, 4 + FC])
        mrows = sb("mrows", [P, 5 * D])

        ps = ctx.enter_context(nc.psum_tensor("ps", [P, 8 * BANK], F32))

        def bank(i, n=BANK, k=1):
            return ps[:, i * BANK:i * BANK + n]

        x_dram = q_x.rearrange("b (t p) d -> p (b t) d", p=P)
        s_x, s_w, s_c, s_prep = sem("x_loaded"), sem("w_loaded"), sem("c_loaded"), sem("prepared")
        s_big = sem("expert_weights_loaded")
        with nc.Block() as block:
            @block.sync
            def _(sp):
                for b in range(B):
                    sp.dma_start(x[:, b * TB:(b + 1) * TB, :], x_dram[:, b * TB:(b + 1) * TB, :]).then_inc(s_x, 16)
                sp.dma_start(bb2s[:, :], bb2).then_inc(s_big, 16)
                for i, w in enumerate((wq, wk, wv)):
                    sp.dma_start(wall[:, i * D:(i + 1) * D], w).then_inc(s_big, 16)
                sp.dma_start(wo_s[:, :], wo).then_inc(s_big, 16)
                sp.dma_start(fc_s[:, :], fc_w).then_inc(s_big, 16)
                sp.dma_start(pj_s[:, :, :], proj_w.rearrange("(c p) d -> p c d", p=P)).then_inc(s_big, 16)
                for i, row in enumerate((bq, bk, bv, bo, proj_b)):
                    sp.dma_start(mrows[:, i * D:(i + 1) * D], row.rearrange("(a d) -> a d", a=1).to_broadcast([P, D])).then_inc(s_big, 16)

            @block.scalar
            def _(act):
                act.dma_start(cst[:, :], consts).then_inc(s_c, 16)
                act.dma_start(wqkv[:, :], w_qkv).then_inc(s_w, 16)
                act.dma_start(w_o_s[:, :], w_o).then_inc(s_w, 16)
                act.dma_start(wg_s[:, :], wg).then_inc(s_w, 16)
                act.dma_start(by_feature[0:E * FC, :], bb1.rearrange("e (c p) -> (e c) p", p=P)).then_inc(s_w, 16)
                for i, row in enumerate((g1, b1)):
                    act.dma_start(by_feature[E * FC + i:E * FC + i + 1, :], row.rearrange("(a d) -> a d", a=1)).then_inc(s_w, 16)
                for i, row in enumerate((ln1_w, ln1_b, ln2_w, ln2_b)):
                    act.dma_start(by_feature2[i:i + 1, :], row.rearrange("(a d) -> a d", a=1)).then_inc(s_w, 16)
                act.dma_start(by_feature2[4:4 + FC, :], fc_b.rearrange("(c p) -> c p", p=P)).then_inc(s_w, 16)
                for i, row in enumerate((g1, b1, g2, b2)):
                    act.dma_start(rows[:, i, :], row.rearrange("(a d) -> a d", a=1).to_broadcast([P, D])).then_inc(s_w, 16)

            @block.vector
            def _(dve):
                dve.wait_ge(s_c, 16)
                nc.vector.tensor_copy(identb[:, :], ident)
                nc.vector.tensor_copy(maskb[:, :], cst[:, P:2 * P])
                nc.vector.memset(wqk[:, :, :, :], 0.0).then_inc(s_prep, 1)
                dve.wait_ge(s_prep, 1)
                dve.wait_ge(s_w, 16 * 15)
                for g in range(NG):
                    for qk in range(2):
                        src = wqkv[:, qk * D + g * 32:qk * D + g * 32 + 32].rearrange("p (j c) -> p j c", j=G4)
                        dst = wqk[:, g, qk, :].rearrange("p (j c) -> p j c", j=G4)
                        for r in range(3):
                            nc.vector.tensor_copy(dst[:, :, r * HD:(r + 1) * HD], src)
                nc.vector.tensor_scalar(rows[:, 2:4, :], rows[:, 2:4, :], 0.5, None, ALU.mult)
                dve.wait_ge(s_prep, 2)
                nc.vector.tensor_copy(fcols[:, :], bank(0, E * FC + 2))
                nc.vector.tensor_copy(mcols[:, :], bank(1, 4 + FC)).then_inc(s_prep, 1)

            @block.tensor
            def _(pe):
                pe.wait_ge(s_c, 16)
                pe.wait_ge(s_w, 16 * 15)
                pe.wait_ge(s_prep, 1)
                nc.tensor.transpose(bank(1, 4 + FC), by_feature2[:, :], cst[0:4 + FC, 0:4 + FC])
                nc.tensor.transpose(bank(0, E * FC + 2), by_feature[:, :], cst[0:E * FC + 2, 0:E * FC + 2]).then_inc(s_prep, 1)

        st6 = sb("st6", [P, 4, 6])
        mv = sb("mv", [P, 2, 4, 2])
        ve = sb("ve", [P, 2, 4])
        sd = sb("sd", [P, 2, 4])

        def stats(dve, source, par):
            for t in range(4):
                nc.vector.bn_stats(st6[:, t, :], source(t))
            dve.drain()
            for t in range(4):
                nc.vector.bn_aggr(mv[:, par, t, :], st6[:, t, :])
            dve.drain()
            return nc.vector.tensor_scalar(ve[:, par, :], mv[:, par, :, 1], EPS, None, ALU.add)

        def credit(eng, *sems):
            for s in sems:
                eng.sem_inc(s, 2)

        def now(eng, s, n):
            eng.wait_ge(s, n + 3)

        def before(eng, s, n):
            eng.wait_ge(s, n + 1)

        def quads(eng, body):
            with eng.Fori(0, QUAD // 2) as i:
                body(i * 2)

        def tiles(t, n):
            return t[:, bass.ds(n * 4, 4), :]

        def tile(t, n, k):
            return t[:, bass.ds(n * 4 + k, 1), :].rearrange("p a d -> p (a d)")

        def wide(row):
            return row.rearrange("p (a d) -> p a d", a=1).to_broadcast([P, 4, row.shape[-1]])

        def quad(i):
            return bank(i).rearrange("p (a d) -> p a d", a=4)

        def turn(i, source):
            for t in range(4):
                last = nc.tensor.transpose(ps[:, i * BANK + t * P:i * BANK + (t + 1) * P], source(t), ident)
            return last

        def normalise(dve, par, out_tile, in_tile):
            nc.vector.reciprocal(ve[:, par, :], sd[:, par, :])
            dve.drain()
            for t in range(4):
                last = nc.vector.tensor_scalar(out_tile(t), in_tile(t), mv[:, par, t, 0:1], ve[:, par, t:t + 1],
                                               ALU.subtract, ALU.mult)
            return last

        def ffn(tag):
            first_norm(tag)
            attention(tag)
            with ExitStack() as mine:
                buffers["w1"] = mine.enter_context(nc.sbuf_tensor(f"{tag}_w1", [P, E, F], F32))
                buffers["w2"] = mine.enter_context(nc.sbuf_tensor(f"{tag}_w2", [P, E, FC, D], F32))
                buffers["loaded"] = sem(f"{tag}_experts_loaded")
                after_attention(tag)
                route(tag)
                experts(tag)

        def attention(tag):
            with ExitStack() as mine:
                attention_of(tag, mine)

        def attention_of(tag, mine):
            def own(name, shape, dt=F32):
                return mine.enter_context(nc.sbuf_tensor(f"{tag}_{name}", shape, dt))

            xt = own("xt", [P, N])
            raw = own("raw", [P, 2, BANK])
            taken = own("taken", [P, BANK])
            qa = own("qa", [P, N], F32R)
            qpad = own("qpad", [P, 2, 2, G4, BANK], F32R)
            mrow = own("mrow", [P, 2, BANK], F32R)
            ka = own("ka", [P, NG, N], F32R)
            va = own("va", [P, NG, TB, G4, STRIP])
            partial = own("partial", [P, 4, 2, G4])
            mcat = own("mcat", [P, TB, P])
            pt = own("pt", [P, SLOTS, G4, BANK])
            ot = own("ot", [P, 2, BANK])
            rs = own("rs", [P, 2, 4, G4])

            unit_full, unit_done = sem(f"{tag}_unit_full"), sem(f"{tag}_unit_done")
            bank_full, bank_done = sem(f"{tag}_bank_full"), sem(f"{tag}_bank_done")
            split, masked, joined = sem(f"{tag}_split"), sem(f"{tag}_masked"), sem(f"{tag}_joined")
            pv_done, sum_out = sem(f"{tag}_pv_done"), sem(f"{tag}_sum_out")
            xt_ready = sem(f"{tag}_xt_ready")
            q_loaded, m_loaded, m_used = sem(f"{tag}_q_loaded"), sem(f"{tag}_m_loaded"), sem(f"{tag}_m_used")
            q_free, q_used, zeroed = sem(f"{tag}_q_free"), sem(f"{tag}_q_used"), sem(f"{tag}_zeroed")
            LOAD = 16 * G4

            def passes(eng, walk):
                walk(PROLOGUE, None)
                with eng.Fori(0, B - 1) as b:
                    walk(BODY, b)
                walk(LAST_BODY, B - 1)

            def bases(b):
                if b is None:
                    return 0, 0, 0, 0, 0, 0
                return (b * BODY_UNITS + PRO_UNITS, b * BODY_EXPS + PRO_EXPS, b * GROUPS_PV, b * (2 * NG), b * NG + 1,
                        b * (8 * NG))

            def where(sched):
                return {(it.step, it.kind, it.x): it.du for it in sched if it.kind == "MT"}

            def unit_at(it, b):
                return ((it.du + (0 if b is None else PRO_UNITS)) % 2) * UNIT_BANKS * BANK

            def bank_at(it, k=0):
                return 2 * UNIT_BANKS + (it.eu + k) % EXP_BANKS

            def products_before(sched, it):
                if it.x == 1:
                    return max([o.eu + 2 for o in sched if o.kind == "ST" and o.step < it.step], default=0)
                return max(o.eu + 2 for o in sched if o.kind == "ST" and o.step == it.step and o.x[0] == 0)

            def diagonal(half, j):
                return P * j >= BANK * half

            def group_of(it, b, ahead):
                if b is None:
                    return it.step + ahead, it.step + ahead
                return (it.step + ahead) % NG, b * NG + it.step + ahead

            with nc.Block() as block:
                @block.tensor
                def _(pe):
                    pe.sem_inc(pv_done, SLOTS)

                    def walk(sched, b):
                        u0, e0, q0, m0, j0, k0 = bases(b)
                        turned = where(sched)
                        pv = {}
                        q = m = m_ot = masks = 0
                        for it in sched:
                            if it.kind == "ST" and it.y == 1:
                                pv[(it.step, *it.x)] = it.eu + 1
                        for it in sched:
                            if it.du is not None:
                                lo = unit_at(it, b)
                                if b is not None or it.du >= 2:
                                    pe.wait_ge(unit_done, u0 + it.du - 1)
                            if it.kind == "P":
                                g, n = group_of(it, b, 2)
                                if (it.x, it.y) == (0, 0) and g == 0:
                                    pe.wait_ge(xt_ready, 16 if b is None else (b + 2) * 16)
                                pe.wait_ge(bank_done, e0 + it.eu + 1)
                                nc.tensor.matmul(bank(bank_at(it)), wqk[:, g, it.x, :], xt[:, it.y * BANK:(it.y + 1) * BANK],
                                                 start=True, stop=True).then_inc(bank_full, 1)
                            elif it.kind == "V":
                                g, n = group_of(it, b, 2)
                                pe.wait_ge(bank_done, e0 + it.eu + 1)
                                for t in range(4):
                                    tok = (4 * it.x + t) * P
                                    last = nc.tensor.matmul(ps[:, bank_at(it) * BANK + t * STRIP:bank_at(it) * BANK + (t + 1) * STRIP],
                                                            xt[:, tok:tok + P], wqkv[:, 2 * D + g * 32:2 * D + g * 32 + 32],
                                                            start=True, stop=True)
                                last.then_inc(bank_full, 1)
                            elif it.kind == "S":
                                g, n = group_of(it, b, 1)
                                i, x = it.x
                                kk0, kk1 = scores(i, x)
                                if i == 0 and it.y == 0:
                                    pe.wait_ge(split, n * 4 + 8)
                                if i in (0, 4) and it.y == 0:
                                    pe.wait_ge(q_loaded, (n * 2 + i // 4 + 1) * LOAD)
                                on_diagonal = kk1 == (i + 1) * P
                                for a in range(2):
                                    last = nc.tensor.matmul(ps[:, lo + a * BANK:lo + a * BANK + kk1 - kk0],
                                                            qpad[:, g % 2, i // 4, 2 * it.y + a, (i % 4) * P:(i % 4 + 1) * P],
                                                            ka[:, g, kk0:kk1], start=True, stop=not on_diagonal)
                                if on_diagonal:
                                    for a in range(2):
                                        col = lo + a * BANK + i * P - kk0
                                        last = nc.tensor.matmul(ps[:, col:col + P], identb[:, :], maskb[:, :], start=False, stop=True)
                                last.then_inc(unit_full, 1)
                            elif it.kind == "MT":
                                if it.x == 0:
                                    pe.wait_ge(unit_done, u0 + it.du - 3)
                                else:
                                    pe.wait_ge(joined, j0 + it.step)
                                for t in range(4):
                                    last = nc.tensor.transpose(ps[:, lo + t * P:lo + (t + 1) * P], mcat[:, 4 * it.x + t, :], ident)
                                last.then_inc(unit_full, 1)
                            elif it.kind == "OT":
                                pe.wait_ge(sum_out, m0 + m_ot + 2)
                                for t in range(4):
                                    last = nc.tensor.transpose(ps[:, lo + t * P:lo + (t + 1) * P],
                                                               ot[:, m_ot % 2, t * P:(t + 1) * P], ident)
                                last.then_inc(unit_full, 1)
                                m_ot += 1
                            elif it.kind == "ST":
                                half, j = it.x
                                g = it.step
                                c0, width = width_of(half, j)
                                if j == 0 and it.y == 0:
                                    pe.wait_ge(m_loaded, ((b * NG + g) * 2 + half + 1) * LOAD)
                                pe.wait_ge(bank_done, e0 + it.eu + 2)
                                for a in range(2):
                                    nc.tensor.matmul(bank(bank_at(it, a), width), ka[:, g, j * P:(j + 1) * P],
                                                     qpad[:, g % 2, half, 2 * it.y + a, c0 - BANK * half:c0 - BANK * half + width],
                                                     start=True, stop=True).then_inc(bank_full, 1)
                            elif it.kind == "PV":
                                half, j = it.x, it.y
                                c0, width = width_of(half, j)
                                pe.wait_ge(bank_done, e0 + pv[(it.step, half, j)] + 4)
                                if diagonal(half, j):
                                    masks += 1
                                    pe.wait_ge(masked, k0 + masks)
                                if j == 0:
                                    pe.wait_ge(sum_out, m0 + m + 1)
                                final = j == 4 * half + 3
                                for h in range(G4):
                                    col = SUM_BANK * BANK + c0 - BANK * half
                                    last = nc.tensor.matmul(ps[STRIP * h:STRIP * (h + 1), col:col + width],
                                                            va[:, it.step, j, h, :], pt[:, q % SLOTS, h, 0:width],
                                                            start=j == 0, stop=final)
                                last.then_inc(pv_done, 1)
                                q += 1
                                m += final

                    passes(pe, walk)

                @block.scalar
                def _(act):
                    act.sem_inc(bank_done, EXP_BANKS)
                    act.sem_inc(sum_out, 1)

                    def walk(sched, b):
                        u0, e0, q0, m0, j0, k0 = bases(b)
                        st = pv = m = 0
                        for it in sched:
                            if it.kind == "P":
                                g, n = group_of(it, b, 2)
                                act.wait_ge(bank_full, e0 + it.eu + 1)
                                act.wait_ge(split, n * 4 + 2 * it.x + it.y + 3)
                                dst, src = raw[:, it.y, :], bank(bank_at(it))
                                if it.x == 0:
                                    nc.scalar.activation(dst, src, ACT.Copy).then_inc(bank_done, 1)
                                else:
                                    nc.scalar.activation(dst, src, ACT.Identity, bias=one_row).then_inc(bank_done, 1)
                            elif it.kind == "V":
                                g, n = group_of(it, b, 2)
                                act.wait_ge(bank_full, e0 + it.eu + 1)
                                nc.scalar.activation(va[:, g, 4 * it.x:4 * it.x + 4, :, 0:HD],
                                                     bank(bank_at(it), 4 * STRIP).rearrange("p (t h c) -> p t h c", t=4, h=G4),
                                                     ACT.Copy).then_inc(bank_done, 1)
                            elif it.kind == "ST":
                                _, width = width_of(*it.x)
                                if it.y == 0:
                                    act.wait_ge(pv_done, q0 + st + 1)
                                for a in range(2):
                                    act.wait_ge(bank_full, e0 + it.eu + a + 1)
                                    nc.scalar.activation(pt[:, st % SLOTS, 2 * it.y + a, 0:width], bank(bank_at(it, a), width),
                                                         ACT.Exp, scale=SCALE).then_inc(bank_done, 1)
                                st += it.y
                            elif it.kind == "PV":
                                pv += 1
                                if it.y == 4 * it.x + 3:
                                    act.wait_ge(pv_done, q0 + pv + SLOTS)
                                    nc.scalar.activation(ot[:, m % 2, :], bank(SUM_BANK), ACT.Copy).then_inc(sum_out, 1)
                                    m += 1

                    passes(act, walk)

                @block.vector
                def _(dve):
                    nc.vector.memset(mcat[:, :, :], 0.0)
                    dve.drain()

                    def walk(sched, b):
                        u0, e0, q0, m0, j0, k0 = bases(b)
                        for n, it in enumerate(sched):
                            if it.du is None:
                                continue
                            lo = unit_at(it, b)
                            dve.wait_ge(unit_full, u0 + it.du + 1)
                            if it.kind == "S":
                                i, x = it.x
                                kk0, kk1 = scores(i, x)
                                if i < 4:
                                    dst = mcat[:, i, :].rearrange("p (h c) -> p h c", h=G4)[:, 2 * it.y:2 * it.y + 2, ONE_ROW]
                                else:
                                    dst = partial[:, i - 4, x, 2 * it.y:2 * it.y + 2]
                                both = ps[:, lo:lo + 2 * BANK].rearrange("p (a k) -> p a k", a=2)[:, :, 0:kk1 - kk0]
                                nc.vector.tensor_reduce(dst, both, AX.X, ALU.max, negate=True).then_inc(unit_done, 1)
                                if (i, x, it.y) == (TB - 1, 1, 1):
                                    dve.drain()
                                    nc.vector.tensor_tensor(
                                        mcat[:, 4:TB, :].rearrange("p t (h c) -> p t h c", h=G4)[:, :, :, ONE_ROW],
                                        partial[:, :, 0, :], partial[:, :, 1, :], ALU.min).then_inc(joined, 1)
                            elif it.kind == "MT":
                                n = it.step + 1 - it.x if b is None else b * NG + it.step + 1 - it.x
                                dve.wait_ge(m_used, n * 2 + it.x + 1)
                                nc.vector.tensor_copy(mrow[:, it.x, :], ps[:, lo:lo + BANK]).then_inc(unit_done, 1)
                            elif it.kind == "OT":
                                half, g = it.x, it.step + it.y
                                turned = ps[:, lo:lo + BANK].rearrange("p (t h c) -> p t h c", t=4, h=G4)
                                nc.vector.reciprocal(rs[:, half, :, :], turned[:, :, :, HD])
                                dve.drain()
                                dst = o[:, bass.ds(b * TB + 4 * half, 4), g * 32:g * 32 + 32]
                                nc.vector.tensor_tensor(
                                    dst.rearrange("p t (h c) -> p t h c", h=G4), turned[:, :, :, 0:HD],
                                    rs[:, half, :, :].rearrange("p t (h a) -> p t h a", a=1).to_broadcast([P, 4, G4, HD]),
                                    ALU.mult).then_inc(unit_done, 1)

                    passes(dve, walk)

                @block.sync
                def _(sp):
                    sp.sem_inc(m_used, 2)
                    sp.sem_inc(q_used, 2)
                    sp.dma_start(xt[:, :], ft[:, 0:N]).then_inc(xt_ready, 16)

                    def load_queries(n, parity, half, read=None):
                        if read is not None:
                            sp.wait_ge(bank_full, read)
                            sp.sem_inc(q_free, 1)
                        sp.wait_ge(split, n * 4 + half + 5)
                        for h in range(G4):
                            s = slice(STRIP * h, STRIP * h + STRIP)
                            sp.dma_start(qpad[s, parity, half, h, :].bitcast(F32), qa[s, half * BANK:(half + 1) * BANK].bitcast(F32)).then_inc(q_loaded, 16)
                        sp.wait_ge(q_loaded, (n * 2 + half + 1) * LOAD)
                        sp.sem_inc(q_used, 1)

                    def load_maxima(n, parity, half):
                        for h in range(G4):
                            s = slice(STRIP * h + ONE_ROW, STRIP * h + ONE_ROW + 1)
                            sp.dma_start(qpad[s, parity, half, h, :].bitcast(F32), mrow[s, half, :].bitcast(F32)).then_inc(m_loaded, 16)
                        sp.wait_ge(m_loaded, (n * 2 + half + 1) * LOAD)
                        sp.sem_inc(m_used, 1)

                    def walk(sched, b):
                        u0, e0, q0, m0, j0, k0 = bases(b)
                        for it in sched:
                            g, n = group_of(it, b, 0)
                            if it.kind == "Z":
                                sp.wait_ge(zeroed, 1)
                                load_queries(0, 0, 0)
                                load_queries(0, 0, 1)
                            elif it.kind == "L" and it.x == 1:
                                load_queries(n + 1, (g + 1) % 2, 1, e0 + products_before(sched, it))
                            elif it.kind == "L":
                                load_queries(n + 2, g % 2, 0, None if b is None else e0 + products_before(sched, it))
                            elif it.kind == "MT":
                                sp.wait_ge(unit_done, u0 + it.du + 1)
                                load_maxima(n + 1 - it.x, (g + 1 - it.x) % 2, it.x)
                            elif it.kind == "V" and it.x == 1 and it.step == 1 and sched is BODY:
                                sp.wait_ge(bank_full, e0 + it.eu + 1)
                                sp.dma_start(xt[:, :], ft[:, bass.ds(b * N + N, N)]).then_inc(xt_ready, 16)

                    passes(sp, walk)

                @block.gpsimd
                def _(pool):
                    pool.sem_inc(split, 4)
                    nc.gpsimd.memset(qpad[:, :, :, :, :].bitcast(F32), 0.0).then_inc(zeroed, 1)
                    nc.gpsimd.memset(va[:, :, :, :, HD:HD + 1], 1.0)
                    nc.gpsimd.memset(va[:, :, :, :, HD + 1:], 0.0)

                    def walk(sched, b):
                        u0, e0, q0, m0, j0, k0 = bases(b)
                        turned = where(sched)
                        for it in sched:
                            if it.kind == "P":
                                g, n = group_of(it, b, 2)
                                pool.wait_ge(bank_done, e0 + it.eu + 4)
                                if it.x == 0:
                                    pool.wait_ge(q_used, n * 2 + it.y + 1)
                                cols = slice(it.y * BANK, (it.y + 1) * BANK)
                                src, coef = raw[:, it.y, :], (coef_q, coef_k)[it.x]
                                dst = qa[:, cols] if it.x == 0 else ka[:, g, cols]
                                nc.gpsimd.tensor_tensor(dst, src, one.to_broadcast([P, BANK]), ALU.mult)
                                pool.drain()
                                nc.gpsimd.tensor_scalar(taken[:, :], dst, coef, None, ALU.mult)
                                pool.drain()
                                nc.gpsimd.tensor_tensor(dst, taken[:, :], src, ALU.add).then_inc(split, 1)
                            elif it.kind == "ST" and it.y == 1 and diagonal(*it.x):
                                q = QUEUE.index(it.x)
                                pool.wait_ge(bank_done, e0 + it.eu + 1 + 4)
                                corner = pt[:, q % SLOTS, :, 0:P]
                                nc.gpsimd.tensor_tensor(gate[:, :], one, one, ALU.mult)
                                pool.drain()
                                nc.gpsimd.affine_select(out=corner, in_=corner, compare_op=ALU.is_ge, fill=0.0, base=0,
                                                        pattern=[[0, G4], [1, P]], channel_multiplier=-1).then_inc(masked, 1)

                    passes(pool, walk)

        def scope(fn):
            def run(tag):
                with ExitStack() as mine:
                    def own(name, shape, dt=F32):
                        return mine.enter_context(nc.sbuf_tensor(f"{tag}_{fn.__name__}_{name}", shape, dt))
                    fn(tag, own, lambda name: sem(f"{tag}_{fn.__name__}_{name}"))
            return run

        @scope
        def first_norm(tag, own, sem):
            xs = own("xs", [P, 2, 4, D])
            var, dev, norm, turned, out_, copied = map(sem, ("var", "dev", "norm", "turned", "evacuated", "copied"))
            with nc.Block() as block:
                @block.vector
                def _(dve):
                    credit(dve, norm)
                    if tag == "f1":
                        dve.wait_ge(s_x, 16 * B)

                    def body(n0):
                        for par in range(2):
                            n = n0 + par
                            stats(dve, lambda t: tile(x, n, t), par).then_inc(var, 1)
                        for par in range(2):
                            n = n0 + par
                            dve.wait_ge(dev, n + 1)
                            before(dve, turned, n)
                            before(dve, copied, n)
                            normalise(dve, par, lambda t: xs[:, par, t, :], lambda t: tile(x, n, t)).then_inc(norm, 1)
                    quads(dve, body)

                @block.scalar
                def _(act):
                    credit(act, out_)

                    def body(n0):
                        for par in range(2):
                            act.wait_ge(var, n0 + par + 1)
                            nc.scalar.activation(sd[:, par, :], ve[:, par, :], ACT.Sqrt).then_inc(dev, 1)
                        for par in range(2):
                            now(act, turned, n0 + par)
                            nc.scalar.activation(ft[:, bass.ds((n0 + par) * BANK, BANK)], bank(par), ACT.Copy).then_inc(out_, 1)
                    quads(act, body)

                @block.tensor
                def _(pe):
                    credit(pe, turned)

                    def body(n0):
                        for par in range(2):
                            now(pe, norm, n0 + par)
                            before(pe, out_, n0 + par)
                            turn(par, lambda t: xs[:, par, t, :]).then_inc(turned, 1)
                    quads(pe, body)

                @block.gpsimd
                def _(pool):
                    credit(pool, copied)

                    def body(n0):
                        for par in range(2):
                            now(pool, norm, n0 + par)
                            nc.gpsimd.tensor_copy(tiles(xn, n0 + par), xs[:, par, :, :]).then_inc(copied, 1)
                    quads(pool, body)

        @scope
        def after_attention(tag, own, sem):
            mid = tag == "mid"
            os_, ots = own("o", [P, 2, 4, D]), own("ot", [P, 2, BANK])
            ys, zs, hs = own("y", [P, 2, 4, D]), own("z", [P, 2, 4, D]), own("h", [P, 2, 4, D])
            hts = own("ht", [P, 2, BANK])
            (staged, turned, ot_ready, product, summed, var, dev, norm, turned2, ht_ready, kept, scored, noted,
             gained, entered) = map(sem, ("staged", "turned", "ot_ready", "product", "summed", "var", "dev", "norm",
                                          "turned2", "ht_ready", "kept", "scored", "noted", "gained", "entered"))
            w_out = wo_s if mid else w_o_s
            gain, shift = (mcols[:, 2:3], mcols[:, 3:4]) if mid else (fcols[:, E * FC:E * FC + 1], fcols[:, E * FC + 1:E * FC + 2])

            with nc.Block() as block:
                if not mid:
                    @block.sync
                    def _(sp):
                        for e in range(E):
                            sp.dma_start(buffers["w1"][:, e, :], w1[e]).then_inc(buffers["loaded"], 16)
                            sp.dma_start(buffers["w2"][:, e, :, :], w2[e].rearrange("(c p) d -> p c d", p=P)).then_inc(buffers["loaded"], 16)

                @block.gpsimd
                def _(pool):
                    credit(pool, staged, kept, gained, entered)

                    def body(n0):
                        for par in range(2):
                            before(pool, turned, n0 + par)
                            nc.gpsimd.tensor_copy(os_[:, par, :, :], tiles(o, n0 + par)).then_inc(staged, 1)
                        if not mid:
                            for par in range(2):
                                n = n0 + par
                                now(pool, norm, n)
                                now(pool, staged, n)
                                before(pool, entered, n)
                                nc.gpsimd.tensor_tensor(hs[:, par, :, :], zs[:, par, :, :], wide(rows[:, 0, :]), ALU.mult).then_inc(gained, 1)
                                pool.drain()
                                nc.gpsimd.tensor_tensor(hs[:, par, :, :], hs[:, par, :, :], wide(rows[:, 1, :]), ALU.add)
                                pool.drain()
                                nc.gpsimd.tensor_copy(tiles(o, n), hs[:, par, :, :]).then_inc(entered, 1)
                        for par in range(2):
                            n = n0 + par
                            now(pool, ht_ready, n)
                            nc.gpsimd.tensor_copy(ft[:, bass.ds(n * BANK, BANK)], hts[:, par, :]).then_inc(kept, 1)
                    quads(pool, body)

                @block.tensor
                def _(pe):
                    credit(pe, turned, product, turned2, scored)

                    def body(n0):
                        for par in range(2):
                            now(pe, staged, n0 + par)
                            before(pe, ot_ready, n0 + par)
                            turn(par, lambda t: os_[:, par, t, :]).then_inc(turned, 1)
                        for par in range(2):
                            now(pe, ot_ready, n0 + par)
                            before(pe, summed, n0 + par)
                            for t in range(4):
                                last = nc.tensor.matmul(ps[:, (2 + par) * BANK + t * P:(2 + par) * BANK + (t + 1) * P],
                                                        ots[:, par, t * P:(t + 1) * P], w_out[:, :], start=True, stop=True)
                            last.then_inc(product, 1)
                        for par in range(2):
                            now(pe, norm, n0 + par)
                            before(pe, ht_ready, n0 + par)
                            turn(4 + par, lambda t: zs[:, par, t, :]).then_inc(turned2, 1)
                        if not mid:
                            for par in range(2):
                                now(pe, ht_ready, n0 + par)
                                before(pe, noted, n0 + par)
                                for t in range(4):
                                    last = nc.tensor.matmul(ps[:, (6 + par) * BANK + t * E:(6 + par) * BANK + (t + 1) * E],
                                                            hts[:, par, t * P:(t + 1) * P], wg_s[:, :], start=True, stop=True)
                                last.then_inc(scored, 1)
                    quads(pe, body)

                @block.scalar
                def _(act):
                    credit(act, ot_ready, ht_ready)

                    def body(n0):
                        for par in range(2):
                            now(act, turned, n0 + par)
                            before(act, product, n0 + par)
                            nc.scalar.activation(ots[:, par, :], bank(par), ACT.Copy).then_inc(ot_ready, 1)
                        for par in range(2):
                            act.wait_ge(var, n0 + par + 1)
                            nc.scalar.activation(sd[:, par, :], ve[:, par, :], ACT.Sqrt).then_inc(dev, 1)
                        for par in range(2):
                            now(act, turned2, n0 + par)
                            before(act, kept, n0 + par)
                            if not mid:
                                before(act, scored, n0 + par)
                            nc.scalar.activation(hts[:, par, :], bank(4 + par), ACT.Identity, bias=shift, scale=gain).then_inc(ht_ready, 1)
                    quads(act, body)

                @block.vector
                def _(dve):
                    credit(dve, summed, norm, noted)

                    def body(n0):
                        for par in range(2):
                            n = n0 + par
                            now(dve, product, n)
                            y = (lambda t: tile(xn, n, t)) if mid else (lambda t: ys[:, par, t, :])
                            y4 = tiles(xn, n) if mid else ys[:, par, :, :]
                            nc.vector.tensor_tensor(y4, tiles(xn, n), quad(2 + par), ALU.add).then_inc(summed, 1)
                            now(dve, summed, n)
                            if mid:
                                nc.vector.tensor_tensor(y4, y4, wide(mrows[:, 3 * D:4 * D]), ALU.add)
                                dve.drain()
                            stats(dve, y, par).then_inc(var, 1)
                        for par in range(2):
                            n = n0 + par
                            y = (lambda t: tile(xn, n, t)) if mid else (lambda t: ys[:, par, t, :])
                            dve.wait_ge(dev, n + 1)
                            before(dve, turned2, n)
                            if not mid:
                                before(dve, gained, n)
                            normalise(dve, par, lambda t: zs[:, par, t, :], y).then_inc(norm, 1)
                        if not mid:
                            for par in range(2):
                                n = n0 + par
                                now(dve, scored, n)
                                nc.vector.tensor_copy(tiles(wr, n), bank(6 + par, 4 * E).rearrange("p (a e) -> p a e", a=4)).then_inc(noted, 1)
                    quads(dve, body)

        @scope
        def route(tag, own, sem):
            ex, top, rest = own("exp", [P, NT, E]), own("top", [P, NT, 8]), own("rest", [P, NT, E])
            peak, total = own("peak", [P, NT]), own("total", [P, NT])
            wt = own("wt", [E, NT * P])
            centred, expd, shares, turned, wt_ready, biased = map(sem, ("centred", "exp", "shares", "turned", "wt_ready", "biased"))

            def bc(ap):
                return ap.rearrange("p (t a) -> p t a", a=1).to_broadcast([P, NT, E])

            with nc.Block() as block:
                @block.vector
                def _(dve):
                    nc.vector.tensor_reduce(peak[:, :], wr[:, :, :], AX.X, ALU.max)
                    dve.drain()
                    nc.vector.tensor_tensor(ex[:, :, :], wr[:, :, :], bc(peak[:, :]), ALU.subtract).then_inc(centred, 1)
                    dve.wait_ge(expd, 1)
                    for t in range(NT):
                        nc.vector.max(top[:, t, :], ex[:, t, :])
                    dve.drain()
                    nc.vector.memset(top[:, :, 2:8], -1.0)
                    nc.vector.tensor_tensor(total[:, :], top[:, :, 0], top[:, :, 1], ALU.add)
                    dve.drain()
                    for t in range(NT):
                        nc.vector.match_replace(rest[:, t, :], top[:, t, :], ex[:, t, :], 0.0)
                    nc.vector.reciprocal(peak[:, :], total[:, :])
                    dve.drain()
                    nc.vector.tensor_tensor(ex[:, :, :], ex[:, :, :], rest[:, :, :], ALU.subtract)
                    dve.drain()
                    nc.vector.tensor_tensor(wr[:, :, :], ex[:, :, :], bc(peak[:, :]), ALU.mult).then_inc(shares, 1)
                    for n in range(QUAD):
                        dve.wait_ge(turned, n + 1)
                        nc.vector.tensor_copy(wt[:, n * BANK:(n + 1) * BANK], ps[0:E, (n % 4) * BANK:(n % 4 + 1) * BANK]).then_inc(wt_ready, 1)
                    for n in range(QUAD):
                        dve.wait_ge(turned, QUAD + n + 1)
                        nc.vector.tensor_tensor(o[:, 4 * n:4 * n + 4, :], o[:, 4 * n:4 * n + 4, :], quad(4 + n % 4), ALU.add).then_inc(biased, 1)

                @block.scalar
                def _(act):
                    act.wait_ge(centred, 1)
                    nc.scalar.activation(ex[:, :, :], ex[:, :, :], ACT.Exp).then_inc(expd, 1)

                @block.tensor
                def _(pe):
                    pe.wait_ge(shares, 1)
                    for n in range(QUAD):
                        if n >= 4:
                            pe.wait_ge(wt_ready, n - 3)
                        for t in range(4):
                            last = nc.tensor.transpose(ps[0:E, (n % 4) * BANK + t * P:(n % 4) * BANK + (t + 1) * P],
                                                       wr[:, 4 * n + t, :], ident)
                        last.then_inc(turned, 1)
                    if tag == "f1":
                        pe.wait_ge(s_big, 16 * BIG_LOADS)
                    for n in range(QUAD):
                        pe.wait_ge(wt_ready, n + 1)
                        if n >= 4:
                            pe.wait_ge(biased, n - 3)
                        for t in range(4):
                            last = nc.tensor.matmul(ps[:, (4 + n % 4) * BANK + t * P:(4 + n % 4) * BANK + (t + 1) * P],
                                                    wt[:, n * BANK + t * P:n * BANK + (t + 1) * P], bb2s[:, :], start=True, stop=True)
                        last.then_inc(turned, 1)

        @scope
        def experts(tag, own, sem):
            acc, ws = own("acc", [P, 2, 4, D]), own("shares", [P, 2, 4, E])
            h1 = own("h1", [P, 2, FC, BANK])
            w1s, w2s = buffers["w1"], buffers["w2"]
            zs, hs, fs = own("z", [P, 2, 4, D]), own("h", [P, 2, 4, D]), own("f", [P, 2, 4, D])
            (staged, up, gelu, down, summed, var, dev, norm, gained, shifted, added) = map(sem, (
                "staged", "up", "gelu", "down", "summed", "var", "dev", "norm", "gained", "shifted", "added"))
            with nc.Block() as block:
                @block.gpsimd
                def _(pool):
                    credit(pool, staged, gained, shifted)

                    def body(n0):
                        for par in range(2):
                            n = n0 + par
                            before(pool, norm, n)
                            nc.gpsimd.tensor_copy(ws[:, par, :, :], tiles(wr, n))
                            nc.gpsimd.tensor_copy(acc[:, par, :, :], tiles(o, n)).then_inc(staged, 1)
                        for par in range(2):
                            n = n0 + par
                            now(pool, norm, n)
                            before(pool, shifted, n)
                            nc.gpsimd.tensor_tensor(hs[:, par, :, :], zs[:, par, :, :], wide(rows[:, 2, :]), ALU.mult).then_inc(gained, 1)
                            now(pool, gained, n)
                            before(pool, added, n)
                            nc.gpsimd.tensor_tensor(fs[:, par, :, :], hs[:, par, :, :], wide(rows[:, 3, :]), ALU.add).then_inc(shifted, 1)
                    quads(pool, body)

                @block.tensor
                def _(pe):
                    def body(n0):
                        for par in range(2):
                            n = n0 + par
                            for e in range(E + 1):
                                if e < E:
                                    for c in range(FC):
                                        u = (n * E + e) * FC + c
                                        pe.wait_ge(gelu, u + 1)
                                        nc.tensor.matmul(bank(c), w1s[:, e, c * P:(c + 1) * P], ft[:, bass.ds(n * BANK, BANK)],
                                                         start=True, stop=True).then_inc(up, 1)
                                if e:
                                    k = n * E + e - 1
                                    pe.wait_ge(gelu, (k + 1) * FC + 4)
                                    before(pe, summed, k)
                                    for t in range(4):
                                        for c in range(FC):
                                            col = (4 + (e - 1) % 2) * BANK + t * P
                                            last = nc.tensor.matmul(ps[:, col:col + P], h1[:, (e - 1) % 2, c, t * P:(t + 1) * P],
                                                                    w2s[:, e - 1, c, :], start=c == 0, stop=c == FC - 1)
                                    last.then_inc(down, 1)
                    credit(pe, down)
                    pe.wait_ge(buffers["loaded"], 16 * 2 * E)
                    quads(pe, body)

                @block.scalar
                def _(act):
                    act.sem_inc(gelu, 4)

                    def body(n0):
                        for par in range(2):
                            n = n0 + par
                            for e in range(E):
                                before(act, down, n * E + e)
                                for c in range(FC):
                                    act.wait_ge(up, (n * E + e) * FC + c + 1)
                                    nc.scalar.activation(h1[:, e % 2, c, :], bank(c), ACT.Gelu_apprx_tanh,
                                                         bias=fcols[:, e * FC + c:e * FC + c + 1]).then_inc(gelu, 1)
                            act.wait_ge(var, n + 1)
                            nc.scalar.activation(sd[:, par, :], ve[:, par, :], ACT.Sqrt).then_inc(dev, 1)
                    quads(act, body)

                @block.vector
                def _(dve):
                    credit(dve, summed, norm, added)

                    def body(n0):
                        for par in range(2):
                            n = n0 + par
                            now(dve, staged, n)
                            for e in range(E):
                                now(dve, down, n * E + e)
                                for t in range(4):
                                    last = nc.vector.scalar_tensor_tensor(
                                        acc[:, par, t, :], ps[:, (4 + e % 2) * BANK + t * P:(4 + e % 2) * BANK + (t + 1) * P],
                                        ws[:, par, t, e:e + 1], acc[:, par, t, :], ALU.mult, ALU.add)
                                last.then_inc(summed, 1)
                                now(dve, summed, n * E + e)
                            stats(dve, lambda t: acc[:, par, t, :], par).then_inc(var, 1)
                            dve.wait_ge(dev, n + 1)
                            before(dve, gained, n)
                            normalise(dve, par, lambda t: zs[:, par, t, :], lambda t: acc[:, par, t, :]).then_inc(norm, 1)
                        for par in range(2):
                            n = n0 + par
                            now(dve, shifted, n)
                            nc.vector.tensor_tensor(tiles(x, n), tiles(x, n), fs[:, par, :, :], ALU.add).then_inc(added, 1)
                    quads(dve, body)

        @scope
        def project(tag, own, sem):
            xs, zs, zt = own("xs", [P, 2, 4, D]), own("z", [P, 2, 4, D]), own("zt", [P, 2, BANK])
            var, dev, kept, norm, twice, turned, zt_ready, product, out_ = map(sem, (
                "var", "dev", "kept", "norm", "twice", "turned", "zt_ready", "product", "out"))
            qkv = buffers["qkv"]
            with nc.Block() as block:
                @block.vector
                def _(dve):
                    credit(dve, norm, twice)
                    dve.sem_inc(out_, 4)

                    def body(n0):
                        for par in range(2):
                            stats(dve, lambda t: tile(x, n0 + par, t), par).then_inc(var, 1)
                        for par in range(2):
                            n = n0 + par
                            dve.wait_ge(dev, n0 * 2 + par + 1)
                            before(dve, kept, n)
                            normalise(dve, par, lambda t: xs[:, par, t, :], lambda t: tile(x, n, t)).then_inc(norm, 1)
                            now(dve, norm, n)
                            stats(dve, lambda t: xs[:, par, t, :], par).then_inc(var, 1)
                        for par in range(2):
                            n = n0 + par
                            dve.wait_ge(dev, n0 * 2 + 2 + par + 1)
                            before(dve, turned, n)
                            normalise(dve, par, lambda t: zs[:, par, t, :], lambda t: xs[:, par, t, :]).then_inc(twice, 1)
                        for par in range(2):
                            n = n0 + par
                            for t in range(4):
                                dve.wait_ge(product, n * 4 + t + 9)
                                nc.vector.tensor_tensor(tile(qkv, n, t), bank(2 + t, 3 * D), mrows[:, 0:3 * D], ALU.add).then_inc(out_, 1)
                    quads(dve, body)

                @block.scalar
                def _(act):
                    credit(act, zt_ready)

                    def body(n0):
                        for k in range(4):
                            act.wait_ge(var, n0 * 2 + k + 1)
                            nc.scalar.activation(sd[:, k % 2, :], ve[:, k % 2, :], ACT.Sqrt).then_inc(dev, 1)
                        for par in range(2):
                            n = n0 + par
                            now(act, turned, n)
                            act.wait_ge(product, n * 4 + 4)
                            nc.scalar.activation(zt[:, par, :], bank(par), ACT.Identity, bias=mcols[:, 1:2], scale=mcols[:, 0:1]).then_inc(zt_ready, 1)
                    quads(act, body)

                @block.tensor
                def _(pe):
                    credit(pe, turned)
                    pe.sem_inc(product, 8)

                    def body(n0):
                        for par in range(2):
                            now(pe, twice, n0 + par)
                            before(pe, zt_ready, n0 + par)
                            turn(par, lambda t: zs[:, par, t, :]).then_inc(turned, 1)
                        for par in range(2):
                            n = n0 + par
                            now(pe, zt_ready, n)
                            for t in range(4):
                                pe.wait_ge(out_, n * 4 + t + 1)
                                nc.tensor.matmul(bank(2 + t, 3 * D), zt[:, par, t * P:(t + 1) * P], wall[:, :],
                                                 start=True, stop=True).then_inc(product, 1)
                    quads(pe, body)

                @block.gpsimd
                def _(pool):
                    credit(pool, kept)

                    def body(n0):
                        for par in range(2):
                            now(pool, norm, n0 + par)
                            nc.gpsimd.tensor_copy(tiles(xn, n0 + par), xs[:, par, :, :]).then_inc(kept, 1)
                    quads(pool, body)

        @scope
        def linear_attention(tag, own, sem):
            VW = HD + 1
            low, expo, feat = (own(n, [P, 2, 2 * D]) for n in ("low", "exp", "feat"))
            vx = own("vx", [P, 2, H, VW])
            pr1, pr2 = own("pr1", [P, 2, H, HD, VW]), own("pr2", [P, 2, H, VW, HD])
            kv, res = own("kv", [P, 2, HD, VW]), own("res", [P, 2, H, VW])
            den = own("den", [P, 2, H])
            lowered, expd, featured, copied, outer, summed, weighed, done = map(sem, (
                "lowered", "exp", "featured", "copied", "outer", "summed", "weighed", "done"))
            qkv = buffers["qkv"]

            def pairs(eng, body):
                with eng.Fori(0, NT // 2) as i:
                    for par in range(2):
                        body(i * 2 + par, par)

            def one(t, n, a, b):
                return t[:, bass.ds(n, 1), a:b].rearrange("p a d -> p (a d)")

            with nc.Block() as block:
                @block.vector
                def _(dve):
                    credit(dve, lowered, featured, summed, done)

                    def features(n, par):
                        before(dve, weighed, n)
                        nc.vector.tensor_scalar(low[:, par, :], one(qkv, n, 0, 2 * D), 0.0, None, ALU.min).then_inc(lowered, 1)
                        dve.wait_ge(expd, n + 1)
                        nc.vector.scalar_tensor_tensor(feat[:, par, :], one(qkv, n, 0, 2 * D), 0.0, expo[:, par, :], ALU.max, ALU.add).then_inc(featured, 1)

                    def rest(n, par):
                        dve.wait_ge(outer, n + 1)
                        nc.vector.tensor_reduce(kv[:, par, :, :].rearrange("p d e -> p (d e)"),
                                                pr1[:, par, :, :, :].rearrange("p h d e -> p (d e) h"), AX.X, ALU.add).then_inc(summed, 1)
                        now(dve, summed, n)
                        fq = feat[:, par, 0:D].rearrange("p (h a d) -> p h a d", a=1, d=HD)
                        kvt = kv[:, par, :, :].rearrange("p (a d) e -> p a e d", a=1)
                        nc.vector.tensor_tensor(pr2[:, par, :, :, :], fq.to_broadcast([P, H, VW, HD]), kvt.to_broadcast([P, H, VW, HD]),
                                                ALU.mult).then_inc(weighed, 1)
                        now(dve, weighed, n)
                        nc.vector.tensor_reduce(res[:, par, :, :], pr2[:, par, :, :, :], AX.X, ALU.add)
                        dve.drain()
                        nc.vector.tensor_scalar(den[:, par, :], res[:, par, :, HD], 1e-6, None, ALU.add)
                        dve.drain()
                        nc.vector.reciprocal(den[:, par, :], den[:, par, :])
                        dve.drain()
                        nc.vector.tensor_tensor(one(o, n, 0, D).rearrange("p (h e) -> p h e", h=H), res[:, par, :, 0:HD],
                                                den[:, par, :].rearrange("p (h a) -> p h a", a=1).to_broadcast([P, H, HD]),
                                                ALU.mult).then_inc(done, 1)

                    credit(dve, weighed)
                    with dve.Fori(0, NT // 2) as i:
                        features(i * 2, 0)
                        features(i * 2 + 1, 1)
                        rest(i * 2, 0)
                        rest(i * 2 + 1, 1)

                @block.scalar
                def _(act):
                    def body(n, par):
                        now(act, lowered, n)
                        before(act, featured, n)
                        nc.scalar.activation(expo[:, par, :], low[:, par, :], ACT.Exp).then_inc(expd, 1)
                    pairs(act, body)

                @block.gpsimd
                def _(pool):
                    nc.gpsimd.memset(vx[:, :, :, HD:VW], 1.0).then_inc(copied, 1)
                    pool.wait_ge(copied, 1)

                    def body(n, par):
                        nc.gpsimd.tensor_copy(vx[:, par, :, 0:HD], one(qkv, n, 2 * D, 3 * D).rearrange("p (h e) -> p h e", h=H)).then_inc(copied, 1)
                        pool.wait_ge(copied, n + 2)
                        now(pool, featured, n)
                        before(pool, summed, n)
                        fk = feat[:, par, D:2 * D].rearrange("p (h d a) -> p h d a", h=H, a=1)
                        v = vx[:, par, :, :].rearrange("p h (a e) -> p h a e", a=1)
                        nc.gpsimd.tensor_tensor(pr1[:, par, :, :, :], fk.to_broadcast([P, H, HD, VW]), v.to_broadcast([P, H, HD, VW]),
                                                ALU.mult).then_inc(outer, 1)
                    pairs(pool, body)

        @scope
        def mlp(tag, own, sem):
            h1 = own("h1", [P, 2, FC, BANK])
            ys, us = own("y", [P, 2, 4, D]), own("u", [P, 2, 4, D])
            up, gelu, down, summed = map(sem, ("up", "gelu", "down", "summed"))
            with nc.Block() as block:
                @block.tensor
                def _(pe):
                    credit(pe, down)

                    def body(n0):
                        for par in range(2):
                            n = n0 + par
                            for c in range(FC):
                                pe.wait_ge(gelu, n * FC + c + 1)
                                nc.tensor.matmul(bank(c), fc_s[:, c * P:(c + 1) * P], ft[:, bass.ds(n * BANK, BANK)],
                                                 start=True, stop=True).then_inc(up, 1)
                        for par in range(2):
                            n = n0 + par
                            pe.wait_ge(gelu, (n + 1) * FC + 4)
                            before(pe, summed, n)
                            for t in range(4):
                                for c in range(FC):
                                    last = nc.tensor.matmul(ps[:, (4 + par) * BANK + t * P:(4 + par) * BANK + (t + 1) * P],
                                                            h1[:, par, c, t * P:(t + 1) * P], pj_s[:, c, :],
                                                            start=c == 0, stop=c == FC - 1)
                            last.then_inc(down, 1)
                    quads(pe, body)

                @block.scalar
                def _(act):
                    act.sem_inc(gelu, 4)

                    def body(n0):
                        for par in range(2):
                            n = n0 + par
                            before(act, down, n)
                            for c in range(FC):
                                act.wait_ge(up, n * FC + c + 1)
                                nc.scalar.activation(h1[:, par, c, :], bank(c), ACT.Gelu, bias=mcols[:, 4 + c:5 + c]).then_inc(gelu, 1)
                    quads(act, body)

                @block.vector
                def _(dve):
                    credit(dve, summed)

                    def body(n0):
                        for par in range(2):
                            n = n0 + par
                            now(dve, down, n)
                            nc.vector.tensor_tensor(ys[:, par, :, :], tiles(xn, n), quad(4 + par), ALU.add).then_inc(summed, 1)
                            now(dve, summed, n)
                            nc.vector.tensor_tensor(us[:, par, :, :], ys[:, par, :, :], wide(mrows[:, 4 * D:5 * D]), ALU.add)
                            dve.drain()
                            nc.vector.tensor_tensor(tiles(x, n), tiles(x, n), us[:, par, :, :], ALU.add)
                        dve.drain()
                    quads(dve, body)

        def linear_layer(tag):
            with ExitStack() as mine:
                buffers["qkv"] = mine.enter_context(nc.sbuf_tensor(f"{tag}_qkv", [P, NT, 3 * D], F32))
                project(tag)
                linear_attention(tag)
            after_attention(tag)
            mlp(tag)

        buffers = {}
        ffn("f1")
        linear_layer("mid")
        ffn("f2")
        s_out = sem("out_stored")
        with nc.Block() as block:
            @block.sync
            def _(sp):
                sp.dma_start(out.rearrange("b (t p) d -> p (b t) d", p=P), x[:, :, :]).then_inc(s_out, 16)
                sp.wait_ge(s_out, 16)


def constants():
    i = np.arange(P)
    row = i % STRIP
    c = np.zeros((P, 2 * P + 4), np.float32)
    c[:, 0:P] = np.eye(P)
    c[:, P:2 * P] = np.where(i[None, :] > i[:, None], NEG, 0)
    c[:, 2 * P] = np.where((row >= 2 * HD) & (row < 3 * HD), -1, 0)
    c[:, 2 * P + 1] = np.where((row >= HD) & (row < 2 * HD), -1, 0)
    c[:, 2 * P + 2] = row == ONE_ROW
    c[:, 2 * P + 3] = 1
    return c


_INS = ['L0_attn_q_x', 'L0_attn_ln1_w', 'L0_attn_ln1_b', 'L0_attn_wq', 'L0_attn_bq', 'L0_attn_wk', 'L0_attn_bk',
        'L0_attn_wv', 'L0_attn_bv', 'L0_attn_wo', 'L0_attn_bo', 'L0_attn_ln2_w', 'L0_attn_ln2_b', 'L0_attn_fc_w',
        'L0_attn_fc_b', 'L0_attn_proj_w', 'L0_attn_proj_b', 'L0_ffn_w_qkv', 'L0_ffn_w_o', 'L0_ffn_g1', 'L0_ffn_b1',
        'L0_ffn_wg', 'L0_ffn_w1', 'L0_ffn_bb1', 'L0_ffn_w2', 'L0_ffn_bb2', 'L0_ffn_g2', 'L0_ffn_b2']


def kernel(**inputs):
    import concourse.bacc as _bacc
    from concourse.bass_utils import run_bass_kernel_spmd as _run

    nc = _bacc.Bacc("TRN2", target_bir_lowering=False, num_devices=1)
    arrays, args = {}, []
    for name in _INS:
        a = np.ascontiguousarray(inputs[name])
        arrays[f"in_{name}"] = a
        args.append(nc.dram_tensor(f"in_{name}", a.shape, mybir.dt.from_np(a.dtype), kind="ExternalInput").ap())
    arrays["constants"] = constants()
    args.append(nc.dram_tensor("constants", arrays["constants"].shape, F32, kind="ExternalInput").ap())
    args.append(nc.dram_tensor("out_dram", (B, N, D), F32, kind="ExternalOutput").ap())
    program(nc, *args)
    r = _run(nc, [arrays], core_ids=[0])
    return r.results[0]["out_dram"]
```

```python
import math
from collections import namedtuple
from contextlib import ExitStack

import concourse.bass as bass
import numpy as np
from concourse import mybir
from concourse.alu_op_type import AluOpType as ALU

F32 = mybir.dt.float32
F32R = mybir.dt.float32r
BF16 = mybir.dt.bfloat16
ACT = mybir.ActivationFunctionType
AX = mybir.AxisListType

B, N, D, H = 4, 1024, 128, 16
HD = D // H
E, F = 8, 512
P = 128
TB = N // P
NT = B * TB
G4 = 4
NG = H // G4
STRIP = P // G4
FC = F // P
EPS = 1e-5
NEG = -1e30
SCALE = 1.0 / math.sqrt(HD)
BANK = 512
BIG_LOADS = 1 + 3 + 1 + 1 + 1 + 5
ONE_ROW = 3 * HD
QUAD = NT // 4


Item = namedtuple("Item", "step kind x y du eu")
UNIT_BANKS, EXP_BANKS, SUM_BANK = 2, 3, 7
SLOTS = 3


def spread(items, lo=0.0, hi=1.0):
    total, at, out = sum(t for *_, t in items) or 1, 0.0, []
    for kind, x, y, t in items:
        out.append((lo + (hi - lo) * at / total, (kind, x, y)))
        at += t
    return out


def scores(i, x):
    return BANK * x, min((i + 1) * P, BANK * (x + 1))


def maxima_uses():
    def use(i, x, pair):
        k0, k1 = scores(i, x)
        return ("S", (i, x), pair, 2 * (k1 - k0) / 0.96 + 65)
    low = [use(i, 0, pair) for i in range(4) for pair in range(2)]
    high = [use(i, x, pair) for i in range(4, TB) for x in range(2) for pair in range(2)]
    return low + high[:3] + [("MT", 0, 0, 620)] + high[3:]


def width_of(half, j):
    c0 = max(BANK * half, P * j)
    return c0, BANK * (half + 1) - c0


def current_uses():
    groups = [(0, j) for j in range(4)] + [(1, j) for j in range(TB)]
    out = []
    for n, (half, j) in enumerate(groups):
        for pair in range(2):
            out.append(("ST", (half, j), pair, 2 * (width_of(half, j)[1] / 1.2 + 52)))
        if n >= 2:
            out.append(("PV", *groups[n - 2], 0))
        if n == 7:
            out.append(("OT", 0, 0, 0))
    return out + [("PV", *groups[-2], 0), ("PV", *groups[-1], 0)]


def projections(step):
    return ([("P", qk, c, 480) for qk in range(2) for c in range(2)]
            + [("V", pair, 0, 210) for pair in range(4) if step % 2 == 0])


def numbered(steps):
    out, du, eu = [], 0, 0
    for g, items in steps:
        for _, (kind, x, y) in sorted(items, key=lambda it: it[0]):
            uses_unit, banks = kind in ("S", "MT", "OT"), {"ST": 2, "P": 1, "V": 1}.get(kind, 0)
            out.append(Item(g, kind, x, y, du if uses_unit else None, eu if banks else None))
            du += uses_unit
            eu += banks
    return out, du, eu


SIGNAL, BACK = 150, 150


def merged(chains, at, t0):
    out, total = [], [sum(cost_of(it)[1] for it in chain) or 1 for chain, _ in chains]
    place, spent = [0] * len(chains), [0.0] * len(chains)
    while any(place[c] < len(chain) for c, (chain, _) in enumerate(chains)):
        best = None
        for c, (chain, release) in enumerate(chains):
            if place[c] == len(chain):
                continue
            kind, x, y = chain[place[c]]
            start = max(at["pe"], t0 + (release[place[c]] if release else 0))
            if kind in ("S", "MT", "OT"):
                start = max(start, at["unit"][at["units"] % 2])
            if kind in ("ST", "P", "V"):
                start = max(start, at["bank"][at["banks"] % EXP_BANKS])
            if kind == "PV":
                start = max(start, at["pt"][(x, y)])
            key = (start, spent[c] / total[c])
            if best is None or key < best[0]:
                best = key, c, start
        _, c, start = best
        item = kind, x, y = chains[c][0][place[c]]
        pe, other = cost_of(item)
        if kind == "ST":
            start = max(start, at["bank"][(at["banks"] + 1) % EXP_BANKS] - pe / 2)
        at["pe"] = start + pe
        if kind in ("S", "MT", "OT"):
            at["dve"] = max(at["dve"], at["pe"] + SIGNAL) + other
            at["unit"][at["units"] % 2] = at["dve"] + BACK
            at["units"] += 1
        for k in range({"ST": 2, "P": 1, "V": 1}.get(kind, 0)):
            uses = 2 if kind == "ST" else 1
            at["act"] = max(at["act"], start + pe * (k + 1) / uses + SIGNAL) + other / uses
            at["bank"][at["banks"] % EXP_BANKS] = at["act"] + BACK
            at["banks"] += 1
        if kind == "P":
            at["pool"] = max(at["pool"], at["act"] + SIGNAL) + 3300
        if kind == "ST":
            at["pt"][x] = at["act"] + SIGNAL
            if y == 1 and P * x[1] >= BANK * x[0]:
                at["pt"][x] = at["pool"] = max(at["pool"], at["act"] + SIGNAL) + 850
        place[c] += 1
        spent[c] += other
        out.append(item)
    return out


def cost_of(item):
    kind, x, y = item
    if kind == "S":
        k0, k1 = scores(*x)
        return 2 * (k1 - k0) / 2.4 + 107 * (k1 == (x[0] + 1) * P), 2 * (k1 - k0) / 0.96 + 65
    if kind == "ST":
        width = width_of(*x)[1]
        return 2 * width / 2.4, 2 * (width / 1.2 + 52)
    if kind == "PV":
        return 4 * width_of(x, y)[1] / 2.4 + 150, 4 * width_of(x, y)[1] / 2.4
    return {"MT": (500, 620), "OT": (500, 450), "P": (860, 480), "V": (860, 210)}[kind]


def batch_element(last):
    steps = []
    at = {"pe": 0, "dve": 0, "act": 0, "unit": [0, 0], "bank": [0] * EXP_BANKS, "units": 0, "banks": 0, "pt": {}, "pool": 0}
    for g in range(NG):
        t0 = at["pe"]
        units = [("MT", 1, 0)]
        if not (last and g == NG - 1):
            units += [it[:3] for it in maxima_uses()]
        chains = [([it[:3] for it in current_uses()], None), (units, None)]
        if not (last and g >= NG - 2):
            chains.append(([it[:3] for it in projections(g)], [4000, 7000, 11500, 15500, 17000, 18000, 19000, 20000]))
        if g:
            chains.append(([("OT", 1, -1)], [2500]))
        order = [(i / 1000, item) for i, item in enumerate(merged(chains, at, t0))]
        if not (last and g == NG - 1):
            order.append((-1.0, ("L", 1, 0)))
        if not (last and g >= NG - 2):
            order.append((0.8 * len(order) / 1000, ("L", 0, 0)))
        if g == NG - 1:
            order.append((2.0, ("OT", 1, 0)))
            at["units"] += 1
        steps.append((g, order))
    return numbered(steps)


PROLOGUE, PRO_UNITS, PRO_EXPS = numbered([
    (-2, spread(projections(-2)) + [(2.0, ("Z", 0, 0))]),
    (-1, spread(projections(-1), 0, 0.3) + [(0.34, ("L", 0, 0))] + spread(maxima_uses(), 0.35, 1.0))])
BODY, BODY_UNITS, BODY_EXPS = batch_element(False)
LAST_BODY = batch_element(True)[0]
assert BODY_UNITS % 2 == 0 and BODY_EXPS % EXP_BANKS == 0 and PRO_EXPS % EXP_BANKS == 0
QUEUE = [(0, j) for j in range(4)] + [(1, j) for j in range(TB)]
GROUPS_PV = len(QUEUE) * NG
assert 12 % SLOTS == 0


def program(nc, q_x, ln1_w, ln1_b, wq, bq, wk, bk, wv, bv, wo, bo, ln2_w, ln2_b, fc_w, fc_b, proj_w, proj_b,
            w_qkv, w_o, g1, b1, wg, w1, bb1, w2, bb2, g2, b2, consts, out):
    with ExitStack() as ctx:
        def sb(name, shape, dt=F32):
            return ctx.enter_context(nc.sbuf_tensor("sb_" + name, shape, dt))

        def sem(name):
            return ctx.enter_context(nc.semaphore(name))

        x = sb("x", [P, NT, D])
        xn = sb("xn", [P, NT, D])
        o = sb("o", [P, NT, D])
        ft = sb("ft", [P, NT * P])

        cst = sb("cst", [P, 2 * P + 4])
        ident = cst[:, 0:P]
        coef_k, coef_q, one_row, one = (cst[:, 2 * P + i:2 * P + i + 1] for i in range(4))
        gate = sb("gate", [P, 1])
        identb = sb("identb", [P, P], BF16)
        maskb = sb("maskb", [P, P], BF16)

        wqkv = sb("wqkv", [P, 3 * D])
        wqk = sb("wqk", [P, NG, 2, P])
        w_o_s = sb("w_o_s", [P, D])
        wg_s = sb("wg_s", [P, E])
        by_feature = sb("by_feature", [E * FC + 2, P])
        fcols = sb("fcols", [P, E * FC + 2])
        bb2s = sb("bb2s", [E, D])
        rows = sb("rows", [P, 4, D])

        wall = sb("wall", [P, 3 * D])
        wo_s = sb("wo_s", [P, D])
        fc_s = sb("fc_s", [P, F])
        pj_s = sb("pj_s", [P, FC, D])
        by_feature2 = sb("by_feature2", [4 + FC, P])
        mcols = sb("mcols", [P, 4 + FC])
        mrows = sb("mrows", [P, 5 * D])

        ps = ctx.enter_context(nc.psum_tensor("ps", [P, 8 * BANK], F32))

        def bank(i, n=BANK):
            return ps[:, i * BANK:i * BANK + n]

        x_dram = q_x.rearrange("b (t p) d -> p (b t) d", p=P)
        s_x, s_w, s_c, s_prep = sem("x_loaded"), sem("w_loaded"), sem("c_loaded"), sem("prepared")
        s_big = sem("expert_weights_loaded")
        with nc.Block() as block:
            @block.sync
            def _(sp):
                for b in range(B):
                    sp.dma_start(x[:, b * TB:(b + 1) * TB, :], x_dram[:, b * TB:(b + 1) * TB, :]).then_inc(s_x, 16)
                sp.dma_start(bb2s[:, :], bb2).then_inc(s_big, 16)
                for i, w in enumerate((wq, wk, wv)):
                    sp.dma_start(wall[:, i * D:(i + 1) * D], w).then_inc(s_big, 16)
                sp.dma_start(wo_s[:, :], wo).then_inc(s_big, 16)
                sp.dma_start(fc_s[:, :], fc_w).then_inc(s_big, 16)
                sp.dma_start(pj_s[:, :, :], proj_w.rearrange("(c p) d -> p c d", p=P)).then_inc(s_big, 16)
                for i, row in enumerate((bq, bk, bv, bo, proj_b)):
                    sp.dma_start(mrows[:, i * D:(i + 1) * D], row.rearrange("(a d) -> a d", a=1).to_broadcast([P, D])).then_inc(s_big, 16)

            @block.scalar
            def _(act):
                act.dma_start(cst[:, :], consts).then_inc(s_c, 16)
                act.dma_start(wqkv[:, :], w_qkv).then_inc(s_w, 16)
                act.dma_start(w_o_s[:, :], w_o).then_inc(s_w, 16)
                act.dma_start(wg_s[:, :], wg).then_inc(s_w, 16)
                act.dma_start(by_feature[0:E * FC, :], bb1.rearrange("e (c p) -> (e c) p", p=P)).then_inc(s_w, 16)
                for i, row in enumerate((g1, b1)):
                    act.dma_start(by_feature[E * FC + i:E * FC + i + 1, :], row.rearrange("(a d) -> a d", a=1)).then_inc(s_w, 16)
                for i, row in enumerate((ln1_w, ln1_b, ln2_w, ln2_b)):
                    act.dma_start(by_feature2[i:i + 1, :], row.rearrange("(a d) -> a d", a=1)).then_inc(s_w, 16)
                act.dma_start(by_feature2[4:4 + FC, :], fc_b.rearrange("(c p) -> c p", p=P)).then_inc(s_w, 16)
                for i, row in enumerate((g1, b1, g2, b2)):
                    act.dma_start(rows[:, i, :], row.rearrange("(a d) -> a d", a=1).to_broadcast([P, D])).then_inc(s_w, 16)

            @block.vector
            def _(dve):
                dve.wait_ge(s_c, 16)
                nc.vector.tensor_copy(identb[:, :], ident)
                nc.vector.tensor_copy(maskb[:, :], cst[:, P:2 * P])
                nc.vector.memset(wqk[:, :, :, :], 0.0).then_inc(s_prep, 1)
                dve.wait_ge(s_prep, 1)
                dve.wait_ge(s_w, 16 * 15)
                for g in range(NG):
                    for qk in range(2):
                        src = wqkv[:, qk * D + g * 32:qk * D + g * 32 + 32].rearrange("p (j c) -> p j c", j=G4)
                        dst = wqk[:, g, qk, :].rearrange("p (j c) -> p j c", j=G4)
                        for r in range(3):
                            nc.vector.tensor_copy(dst[:, :, r * HD:(r + 1) * HD], src)
                nc.vector.tensor_scalar(rows[:, 2:4, :], rows[:, 2:4, :], 0.5, None, ALU.mult)
                dve.wait_ge(s_prep, 2)
                nc.vector.tensor_copy(fcols[:, :], bank(0, E * FC + 2))
                nc.vector.tensor_copy(mcols[:, :], bank(1, 4 + FC)).then_inc(s_prep, 1)

            @block.tensor
            def _(pe):
                pe.wait_ge(s_c, 16)
                pe.wait_ge(s_w, 16 * 15)
                pe.wait_ge(s_prep, 1)
                nc.tensor.transpose(bank(1, 4 + FC), by_feature2[:, :], cst[0:4 + FC, 0:4 + FC])
                nc.tensor.transpose(bank(0, E * FC + 2), by_feature[:, :], cst[0:E * FC + 2, 0:E * FC + 2]).then_inc(s_prep, 1)

        st6 = sb("st6", [P, 4, 6])
        mv = sb("mv", [P, 2, 4, 2])
        ve = sb("ve", [P, 2, 4])
        sd = sb("sd", [P, 2, 4])

        def stats(dve, source, par):
            for t in range(4):
                nc.vector.bn_stats(st6[:, t, :], source(t))
            dve.drain()
            for t in range(4):
                nc.vector.bn_aggr(mv[:, par, t, :], st6[:, t, :])
            dve.drain()
            return nc.vector.tensor_scalar(ve[:, par, :], mv[:, par, :, 1], EPS, None, ALU.add)

        def credit(eng, *sems):
            for s in sems:
                eng.sem_inc(s, 2)

        def now(eng, s, n):
            eng.wait_ge(s, n + 3)

        def before(eng, s, n):
            eng.wait_ge(s, n + 1)

        def quads(eng, body):
            with eng.Fori(0, QUAD // 2) as i:
                body(i * 2)

        def tiles(t, n):
            return t[:, bass.ds(n * 4, 4), :]

        def tile(t, n, k):
            return t[:, bass.ds(n * 4 + k, 1), :].rearrange("p a d -> p (a d)")

        def wide(row):
            return row.rearrange("p (a d) -> p a d", a=1).to_broadcast([P, 4, row.shape[-1]])

        def quad(i):
            return bank(i).rearrange("p (a d) -> p a d", a=4)

        def turn(i, source):
            for t in range(4):
                last = nc.tensor.transpose(ps[:, i * BANK + t * P:i * BANK + (t + 1) * P], source(t), ident)
            return last

        def normalise(dve, par, out_tile, in_tile):
            nc.vector.reciprocal(ve[:, par, :], sd[:, par, :])
            dve.drain()
            for t in range(4):
                last = nc.vector.tensor_scalar(out_tile(t), in_tile(t), mv[:, par, t, 0:1], ve[:, par, t:t + 1],
                                               ALU.subtract, ALU.mult)
            return last

        def ffn(tag):
            if tag == "f1":
                first_norm(tag)
            attention(tag)
            with ExitStack() as mine:
                buffers["w1"] = mine.enter_context(nc.sbuf_tensor(f"{tag}_w1", [P, E, F], F32))
                buffers["w2"] = mine.enter_context(nc.sbuf_tensor(f"{tag}_w2", [P, E, FC, D], F32))
                buffers["loaded"] = sem(f"{tag}_experts_loaded")
                experts(tag)

        def attention(tag):
            with ExitStack() as mine:
                attention_of(tag, mine)

        def attention_of(tag, mine):
            def own(name, shape, dt=F32):
                return mine.enter_context(nc.sbuf_tensor(f"{tag}_{name}", shape, dt))

            xt = own("xt", [P, N])
            raw = own("raw", [P, 4, BANK])
            taken = own("taken", [P, BANK])
            qa = own("qa", [P, N], F32R)
            qpad = own("qpad", [P, 2, 2, G4, BANK], F32R)
            mrow = own("mrow", [P, 2, BANK], F32R)
            ka = own("ka", [P, NG, N], F32R)
            va = own("va", [P, NG, TB, G4, STRIP])
            partial = own("partial", [P, 4, 2, G4])
            mcat = own("mcat", [P, TB, P])
            pt = own("pt", [P, SLOTS, G4, BANK])
            ot = own("ot", [P, 2, BANK])
            rs = own("rs", [P, 2, 4, G4])

            unit_full, unit_done = sem(f"{tag}_unit_full"), sem(f"{tag}_unit_done")
            bank_full, bank_done = sem(f"{tag}_bank_full"), sem(f"{tag}_bank_done")
            split, masked, joined = sem(f"{tag}_split"), sem(f"{tag}_masked"), sem(f"{tag}_joined")
            pv_done, sum_out = sem(f"{tag}_pv_done"), sem(f"{tag}_sum_out")
            xt_ready = sem(f"{tag}_xt_ready")
            q_loaded, m_loaded, m_used = sem(f"{tag}_q_loaded"), sem(f"{tag}_m_loaded"), sem(f"{tag}_m_used")
            q_free, q_used, zeroed = sem(f"{tag}_q_free"), sem(f"{tag}_q_used"), sem(f"{tag}_zeroed")
            LOAD = 16 * G4

            def passes(eng, walk):
                walk(PROLOGUE, None)
                with eng.Fori(0, B - 1) as b:
                    walk(BODY, b)
                walk(LAST_BODY, B - 1)

            def bases(b):
                if b is None:
                    return 0, 0, 0, 0, 0, 0
                return (b * BODY_UNITS + PRO_UNITS, b * BODY_EXPS + PRO_EXPS, b * GROUPS_PV, b * (2 * NG), b * NG + 1,
                        b * (8 * NG))

            def unit_at(it, b):
                return ((it.du + (0 if b is None else PRO_UNITS)) % 2) * UNIT_BANKS * BANK

            def bank_at(it, k=0):
                return 2 * UNIT_BANKS + (it.eu + k) % EXP_BANKS

            def products_before(sched, it):
                if it.x == 1:
                    return max([o.eu + 2 for o in sched if o.kind == "ST" and o.step < it.step], default=0)
                return max(o.eu + 2 for o in sched if o.kind == "ST" and o.step == it.step and o.x[0] == 0)

            def diagonal(half, j):
                return P * j >= BANK * half

            def group_of(it, b, ahead):
                if b is None:
                    return it.step + ahead, it.step + ahead
                return (it.step + ahead) % NG, b * NG + it.step + ahead

            with nc.Block() as block:
                @block.tensor
                def _(pe):
                    pe.sem_inc(pv_done, SLOTS)

                    def walk(sched, b):
                        u0, e0, q0, m0, j0, k0 = bases(b)
                        pv = {}
                        q = m = m_ot = masks = 0
                        for it in sched:
                            if it.kind == "ST" and it.y == 1:
                                pv[(it.step, *it.x)] = it.eu + 1
                        for it in sched:
                            if it.du is not None:
                                lo = unit_at(it, b)
                                if b is not None or it.du >= 2:
                                    pe.wait_ge(unit_done, u0 + it.du - 1)
                            if it.kind == "P":
                                g, n = group_of(it, b, 2)
                                if (it.x, it.y) == (0, 0) and g == 0:
                                    pe.wait_ge(xt_ready, 16 if b is None else (b + 2) * 16)
                                pe.wait_ge(bank_done, e0 + it.eu + 1)
                                nc.tensor.matmul(bank(bank_at(it)), wqk[:, g, it.x, :], xt[:, it.y * BANK:(it.y + 1) * BANK],
                                                 start=True, stop=True).then_inc(bank_full, 1)
                            elif it.kind == "V":
                                g, n = group_of(it, b, 2)
                                pe.wait_ge(bank_done, e0 + it.eu + 1)
                                for t in range(2):
                                    tok = (2 * it.x + t) * P
                                    col = bank_at(it) * BANK + t * 2 * STRIP
                                    last = nc.tensor.matmul(ps[:, col:col + 64], xt[:, tok:tok + P],
                                                            wqkv[:, 2 * D + g * 32:2 * D + g * 32 + 64], start=True, stop=True)
                                last.then_inc(bank_full, 1)
                            elif it.kind == "S":
                                g, n = group_of(it, b, 1)
                                i, x = it.x
                                kk0, kk1 = scores(i, x)
                                if i == 0 and it.y == 0:
                                    pe.wait_ge(split, n * 4 + 8)
                                if i in (0, 4) and it.y == 0:
                                    pe.wait_ge(q_loaded, (n * 2 + i // 4 + 1) * LOAD)
                                on_diagonal = kk1 == (i + 1) * P
                                for a in range(2):
                                    last = nc.tensor.matmul(ps[:, lo + a * BANK:lo + a * BANK + kk1 - kk0],
                                                            qpad[:, g % 2, i // 4, 2 * it.y + a, (i % 4) * P:(i % 4 + 1) * P],
                                                            ka[:, g, kk0:kk1], start=True, stop=not on_diagonal)
                                if on_diagonal:
                                    for a in range(2):
                                        col = lo + a * BANK + i * P - kk0
                                        last = nc.tensor.matmul(ps[:, col:col + P], identb[:, :], maskb[:, :], start=False, stop=True)
                                last.then_inc(unit_full, 1)
                            elif it.kind == "MT":
                                if it.x == 0:
                                    pe.wait_ge(unit_done, u0 + it.du - 3)
                                else:
                                    pe.wait_ge(joined, j0 + it.step)
                                for t in range(4):
                                    last = nc.tensor.transpose(ps[:, lo + t * P:lo + (t + 1) * P], mcat[:, 4 * it.x + t, :], ident)
                                last.then_inc(unit_full, 1)
                            elif it.kind == "OT":
                                pe.wait_ge(sum_out, m0 + m_ot + 2)
                                for t in range(4):
                                    last = nc.tensor.transpose(ps[:, lo + t * P:lo + (t + 1) * P],
                                                               ot[:, m_ot % 2, t * P:(t + 1) * P], ident)
                                last.then_inc(unit_full, 1)
                                m_ot += 1
                            elif it.kind == "ST":
                                half, j = it.x
                                g = it.step
                                c0, width = width_of(half, j)
                                if j == 0 and it.y == 0:
                                    pe.wait_ge(m_loaded, ((b * NG + g) * 2 + half + 1) * LOAD)
                                for a in range(2):
                                    pe.wait_ge(bank_done, e0 + it.eu + a + 1)
                                    nc.tensor.matmul(bank(bank_at(it, a), width), ka[:, g, j * P:(j + 1) * P],
                                                     qpad[:, g % 2, half, 2 * it.y + a, c0 - BANK * half:c0 - BANK * half + width],
                                                     start=True, stop=True).then_inc(bank_full, 1)
                            elif it.kind == "PV":
                                half, j = it.x, it.y
                                c0, width = width_of(half, j)
                                pe.wait_ge(bank_done, e0 + pv[(it.step, half, j)] + 4)
                                if diagonal(half, j):
                                    masks += 1
                                    pe.wait_ge(masked, k0 + masks)
                                if j == 0:
                                    pe.wait_ge(sum_out, m0 + m + 1)
                                final = j == 4 * half + 3
                                for h in range(G4):
                                    col = SUM_BANK * BANK + c0 - BANK * half
                                    last = nc.tensor.matmul(ps[STRIP * h:STRIP * (h + 1), col:col + width],
                                                            va[:, it.step, j, h, :], pt[:, q % SLOTS, h, 0:width],
                                                            start=j == 0, stop=final)
                                last.then_inc(pv_done, 1)
                                q += 1
                                m += final

                    passes(pe, walk)

                @block.scalar
                def _(act):
                    act.sem_inc(bank_done, EXP_BANKS)
                    act.sem_inc(sum_out, 1)

                    def walk(sched, b):
                        u0, e0, q0, m0, j0, k0 = bases(b)
                        st = pv = m = 0
                        for it in sched:
                            if it.kind == "P":
                                g, n = group_of(it, b, 2)
                                act.wait_ge(bank_full, e0 + it.eu + 1)
                                act.wait_ge(split, n * 4 + 2 * it.x + it.y + 1)
                                dst, src = raw[:, 2 * it.x + it.y, :], bank(bank_at(it))
                                if it.x == 0:
                                    nc.scalar.activation(dst, src, ACT.Copy).then_inc(bank_done, 1)
                                else:
                                    nc.scalar.activation(dst, src, ACT.Identity, bias=one_row).then_inc(bank_done, 1)
                            elif it.kind == "V":
                                g, n = group_of(it, b, 2)
                                act.wait_ge(bank_full, e0 + it.eu + 1)
                                for t in range(2):
                                    col = bank_at(it) * BANK + t * 2 * STRIP
                                    last = nc.scalar.activation(va[:, g:g + 2, 2 * it.x + t, :, 0:HD],
                                                                ps[:, col:col + 64].rearrange("p (g h c) -> p g h c", g=2, h=G4), ACT.Copy)
                                last.then_inc(bank_done, 1)
                            elif it.kind == "ST":
                                _, width = width_of(*it.x)
                                if it.y == 0:
                                    act.wait_ge(pv_done, q0 + st + 1)
                                for a in range(2):
                                    act.wait_ge(bank_full, e0 + it.eu + a + 1)
                                    nc.scalar.activation(pt[:, st % SLOTS, 2 * it.y + a, 0:width], bank(bank_at(it, a), width),
                                                         ACT.Exp, scale=SCALE).then_inc(bank_done, 1)
                                st += it.y
                            elif it.kind == "PV":
                                pv += 1
                                if it.y == 4 * it.x + 3:
                                    act.wait_ge(pv_done, q0 + pv + SLOTS)
                                    nc.scalar.activation(ot[:, m % 2, :], bank(SUM_BANK), ACT.Copy).then_inc(sum_out, 1)
                                    m += 1

                    passes(act, walk)

                @block.vector
                def _(dve):
                    nc.vector.memset(mcat[:, :, :], 0.0)
                    dve.drain()

                    def walk(sched, b):
                        u0, e0, q0, m0, j0, k0 = bases(b)
                        for it in sched:
                            if it.kind == "P" and b is None:
                                g, n = group_of(it, b, 2)
                                dve.wait_ge(bank_done, it.eu + 4)
                                if it.x == 0:
                                    dve.wait_ge(q_used, n * 2 + it.y + 1)
                                cols = slice(it.y * BANK, (it.y + 1) * BANK)
                                src, coef = raw[:, 2 * it.x + it.y, :], (coef_q, coef_k)[it.x]
                                dst = qa[:, cols] if it.x == 0 else ka[:, g, cols]
                                nc.vector.tensor_copy(dst, src)
                                dve.drain()
                                nc.vector.scalar_tensor_tensor(dst, dst, coef, src, ALU.mult, ALU.add).then_inc(split, 1)
                            if it.du is None:
                                continue
                            lo = unit_at(it, b)
                            dve.wait_ge(unit_full, u0 + it.du + 1)
                            if it.kind == "S":
                                i, x = it.x
                                kk0, kk1 = scores(i, x)
                                if i < 4:
                                    dst = mcat[:, i, :].rearrange("p (h c) -> p h c", h=G4)[:, 2 * it.y:2 * it.y + 2, ONE_ROW]
                                else:
                                    dst = partial[:, i - 4, x, 2 * it.y:2 * it.y + 2]
                                both = ps[:, lo:lo + 2 * BANK].rearrange("p (a k) -> p a k", a=2)[:, :, 0:kk1 - kk0]
                                nc.vector.tensor_reduce(dst, both, AX.X, ALU.max, negate=True).then_inc(unit_done, 1)
                                if (i, x, it.y) == (TB - 1, 1, 1):
                                    dve.drain()
                                    nc.vector.tensor_tensor(
                                        mcat[:, 4:TB, :].rearrange("p t (h c) -> p t h c", h=G4)[:, :, :, ONE_ROW],
                                        partial[:, :, 0, :], partial[:, :, 1, :], ALU.min).then_inc(joined, 1)
                            elif it.kind == "MT":
                                n = it.step + 1 - it.x if b is None else b * NG + it.step + 1 - it.x
                                dve.wait_ge(m_used, n * 2 + it.x + 1)
                                nc.vector.tensor_copy(mrow[:, it.x, :], ps[:, lo:lo + BANK]).then_inc(unit_done, 1)
                            elif it.kind == "OT":
                                half, g = it.x, it.step + it.y
                                turned = ps[:, lo:lo + BANK].rearrange("p (t h c) -> p t h c", t=4, h=G4)
                                nc.vector.reciprocal(rs[:, half, :, :], turned[:, :, :, HD])
                                dve.drain()
                                dst = o[:, bass.ds(b * TB + 4 * half, 4), g * 32:g * 32 + 32]
                                nc.vector.tensor_tensor(
                                    dst.rearrange("p t (h c) -> p t h c", h=G4), turned[:, :, :, 0:HD],
                                    rs[:, half, :, :].rearrange("p t (h a) -> p t h a", a=1).to_broadcast([P, 4, G4, HD]),
                                    ALU.mult).then_inc(unit_done, 1)

                    passes(dve, walk)

                @block.sync
                def _(sp):
                    sp.sem_inc(m_used, 2)
                    sp.sem_inc(q_used, 2)
                    sp.dma_start(xt[:, :], ft[:, 0:N]).then_inc(xt_ready, 16)

                    def load_queries(n, parity, half, read=None):
                        if read is not None:
                            sp.wait_ge(bank_full, read)
                            sp.sem_inc(q_free, 1)
                        sp.wait_ge(split, n * 4 + half + 5)
                        for h in range(G4):
                            s = slice(STRIP * h, STRIP * h + STRIP)
                            sp.dma_start(qpad[s, parity, half, h, :].bitcast(F32), qa[s, half * BANK:(half + 1) * BANK].bitcast(F32)).then_inc(q_loaded, 16)
                        sp.wait_ge(q_loaded, (n * 2 + half + 1) * LOAD)
                        sp.sem_inc(q_used, 1)

                    def load_maxima(n, parity, half):
                        for h in range(G4):
                            s = slice(STRIP * h + ONE_ROW, STRIP * h + ONE_ROW + 1)
                            sp.dma_start(qpad[s, parity, half, h, :].bitcast(F32), mrow[s, half, :].bitcast(F32)).then_inc(m_loaded, 16)
                        sp.wait_ge(m_loaded, (n * 2 + half + 1) * LOAD)
                        sp.sem_inc(m_used, 1)

                    def walk(sched, b):
                        u0, e0, q0, m0, j0, k0 = bases(b)
                        for it in sched:
                            g, n = group_of(it, b, 0)
                            if it.kind == "Z":
                                sp.wait_ge(zeroed, 1)
                                load_queries(0, 0, 0)
                                load_queries(0, 0, 1)
                            elif it.kind == "L" and it.x == 1:
                                load_queries(n + 1, (g + 1) % 2, 1, e0 + products_before(sched, it))
                            elif it.kind == "L":
                                load_queries(n + 2, g % 2, 0, None if b is None else e0 + products_before(sched, it))
                            elif it.kind == "MT":
                                sp.wait_ge(unit_done, u0 + it.du + 1)
                                load_maxima(n + 1 - it.x, (g + 1 - it.x) % 2, it.x)
                            elif (it.kind, it.x, it.y, it.step) == ("P", 1, 1, 1) and sched is BODY:
                                sp.wait_ge(bank_full, e0 + it.eu + 1)
                                sp.dma_start(xt[:, :], ft[:, bass.ds(b * N + N, N)]).then_inc(xt_ready, 16)

                    passes(sp, walk)

                @block.gpsimd
                def _(pool):
                    pool.sem_inc(split, 4)
                    nc.gpsimd.memset(qpad[:, :, :, :, :].bitcast(F32), 0.0).then_inc(zeroed, 1)
                    nc.gpsimd.memset(va[:, :, :, :, HD:HD + 1], 1.0)
                    nc.gpsimd.memset(va[:, :, :, :, HD + 1:], 0.0)
                    pool.wait_ge(split, 4 + 8)

                    def walk(sched, b):
                        u0, e0, q0, m0, j0, k0 = bases(b)
                        for it in sched:
                            if it.kind == "P" and b is not None:
                                g, n = group_of(it, b, 2)
                                pool.wait_ge(bank_done, e0 + it.eu + 4)
                                if it.x == 0:
                                    pool.wait_ge(q_used, n * 2 + it.y + 1)
                                cols = slice(it.y * BANK, (it.y + 1) * BANK)
                                src, coef = raw[:, 2 * it.x + it.y, :], (coef_q, coef_k)[it.x]
                                dst = qa[:, cols] if it.x == 0 else ka[:, g, cols]
                                nc.gpsimd.tensor_tensor(dst, src, one.to_broadcast([P, BANK]), ALU.mult)
                                pool.drain()
                                nc.gpsimd.tensor_scalar(taken[:, :], dst, coef, None, ALU.mult)
                                pool.drain()
                                nc.gpsimd.tensor_tensor(dst, taken[:, :], src, ALU.add).then_inc(split, 1)
                            elif it.kind == "ST" and it.y == 1 and diagonal(*it.x):
                                q = QUEUE.index(it.x)
                                pool.wait_ge(bank_done, e0 + it.eu + 1 + 4)
                                corner = pt[:, q % SLOTS, :, 0:P]
                                nc.gpsimd.tensor_tensor(gate[:, :], one, one, ALU.mult)
                                pool.drain()
                                nc.gpsimd.affine_select(out=corner, in_=corner, compare_op=ALU.is_ge, fill=0.0, base=0,
                                                        pattern=[[0, G4], [1, P]], channel_multiplier=-1).then_inc(masked, 1)

                    passes(pool, walk)

        def scope(fn):
            def run(tag):
                with ExitStack() as mine:
                    def own(name, shape, dt=F32):
                        return mine.enter_context(nc.sbuf_tensor(f"{tag}_{fn.__name__}_{name}", shape, dt))
                    fn(tag, own, lambda name: sem(f"{tag}_{fn.__name__}_{name}"))
            return run

        @scope
        def first_norm(tag, own, sem):
            xs = own("xs", [P, 2, 4, D])
            var, dev, norm, turned, out_, copied = map(sem, ("var", "dev", "norm", "turned", "evacuated", "copied"))
            with nc.Block() as block:
                @block.vector
                def _(dve):
                    credit(dve, norm)
                    if tag == "f1":
                        dve.wait_ge(s_x, 16 * B)

                    def body(n0):
                        for par in range(2):
                            n = n0 + par
                            stats(dve, lambda t: tile(x, n, t), par).then_inc(var, 1)
                        for par in range(2):
                            n = n0 + par
                            dve.wait_ge(dev, n + 1)
                            before(dve, turned, n)
                            before(dve, copied, n)
                            normalise(dve, par, lambda t: xs[:, par, t, :], lambda t: tile(x, n, t)).then_inc(norm, 1)
                    quads(dve, body)

                @block.scalar
                def _(act):
                    credit(act, out_)

                    def body(n0):
                        for par in range(2):
                            act.wait_ge(var, n0 + par + 1)
                            nc.scalar.activation(sd[:, par, :], ve[:, par, :], ACT.Sqrt).then_inc(dev, 1)
                        for par in range(2):
                            now(act, turned, n0 + par)
                            nc.scalar.activation(ft[:, bass.ds((n0 + par) * BANK, BANK)], bank(par), ACT.Copy).then_inc(out_, 1)
                    quads(act, body)

                @block.tensor
                def _(pe):
                    credit(pe, turned)

                    def body(n0):
                        for par in range(2):
                            now(pe, norm, n0 + par)
                            before(pe, out_, n0 + par)
                            turn(par, lambda t: xs[:, par, t, :]).then_inc(turned, 1)
                    quads(pe, body)

                @block.gpsimd
                def _(pool):
                    credit(pool, copied)

                    def body(n0):
                        for par in range(2):
                            now(pool, norm, n0 + par)
                            nc.gpsimd.tensor_copy(tiles(xn, n0 + par), xs[:, par, :, :]).then_inc(copied, 1)
                    quads(pool, body)

        CREDIT = 4
        FRONT, A, BB, C = -1, 1, 2, 3

        RING = [(use, part, 6 + i % 2, *event) for i, (use, part, event) in enumerate([
            ("up0", C, ("gelu2", 4, 0)), ("up1", C, ("gelu2", 4, 1)), ("up2", C, ("gelu2", 4, 2)),
            ("turn_f", FRONT, ("otf_ready", 1, 0)), ("up3", C, ("gelu2", 4, 3)), ("prod_f", FRONT, ("f_summed", 1, 0)), ("down", C, ("mlp_summed", 1, 0)),
            ("turn_zf", FRONT, ("htf_ready", 1, 0)), ("turn_o", BB, ("ot_ready", 1, 0)), ("turn_z", A, ("zt_ready", 1, 0)),
            ("logits", FRONT, ("centred", 1, 0)), ("prod_o", BB, ("o_summed", 1, 0)), ("qkv0", A, ("qkv_kept", 4, 0)),
            ("qkv1", A, ("qkv_kept", 4, 1)), ("qkv2", A, ("qkv_kept", 4, 2)), ("qkv3", A, ("qkv_kept", 4, 3)),
            ("turn_w", FRONT, ("wt_ready", 1, 0)), ("turn_x", C, ("xt_kept", 1, 0)), ("turn_z2", BB, ("ht_ready", 1, 0)), ("bias", FRONT, ("prepared", 1, 0))])]

        MLP_CHUNKS = ((0, 1), (2,), (3,))

        def ring_bank(use):
            return next(r[2] for r in RING if r[0] == use)

        def freed_by(use, parts, parts_before):
            i = next(i for i, r in enumerate(RING) if r[0] == use)
            for later, on, rows_ in ((0, parts, RING[:i]), (1, parts_before, RING)):
                for _, part, bank_, event, per, k in reversed(rows_):
                    if part in on and bank_ == RING[i][2]:
                        return event, per, k, part + later
            return None

        @scope
        def experts(tag, own, sem):
            linear = tag == "f1"
            VW = HD + 1
            acc, ws = own("acc", [P, 2, 4, D]), own("shares", [P, 2, 4, E])
            h1 = own("h1", [P, 2, FC, BANK])
            w1s, w2s = buffers["w1"], buffers["w2"]
            ze, gs, fs = own("ze", [P, 4, D]), own("gs", [P, 4, D]), own("fs", [P, 4, D])
            osf, otf, zf = own("osf", [P, 4, D]), own("otf", [P, BANK]), own("zf", [P, 4, D])
            hs, htf, wt = own("hs", [P, 4, D]), own("htf", [P, BANK]), own("wt", [E, BANK])
            ex, top, rest = own("ex", [P, 4, E]), own("top", [P, 4, 8]), own("rest", [P, 4, E])
            peak, total = own("peak", [P, 4]), own("total", [P, 4])
            mvs, ves, sds = own("mvs", [P, 6, 4, 2]), own("ves", [P, 6, 4]), own("sds", [P, 6, 4])
            s = {}
            for name in ("up", "gelu", "down", "summed", "gained", "shifted", "added", "var0", "dev0", "norm0",
                         "var4", "dev4", "norm4", "staged", "turned_f", "otf_ready", "f_product", "f_summed", "turned_zf",
                         "htf_ready", "scored", "centred", "ex_ready", "shares", "turned_w", "wt_ready", "bias_product",
                         "h_gained", "h_ready", "prepared"):
                s[name] = sem(name)
            if linear:
                z, zt = own("z", [P, 4, D]), own("zt", [P, BANK])
                qk, low, feat = (own(n, [P, 4, 2 * D]) for n in ("qk", "low", "feat"))
                vx = own("vx", [P, 4, H, VW])
                pr1, pr2 = own("pr1", [P, 2, H, HD, VW]), own("pr2", [P, H, VW, HD])
                kv, res, den = own("kv", [P, HD, VW]), own("res", [P, H, VW]), own("den", [P, H])
                os_, ot, z2, ht = own("os", [P, 4, D]), own("ot", [P, BANK]), own("z2", [P, 4, D]), own("ht", [P, BANK])
                h2, ys, zx = own("h2", [P, FC, BANK]), own("y", [P, 4, D]), own("zx", [P, 4, D])
                for name in ("var1", "dev1", "norm1", "var2", "dev2", "norm2", "var3", "dev3", "norm3", "turned_z",
                             "zt_ready", "product", "qkv_kept", "lowered", "expd", "featured", "outer", "kv_summed",
                             "weighed", "o_made", "turned_o", "ot_ready", "o_product", "o_summed", "turned_z2", "ht_ready",
                             "up2", "gelu2", "down2", "mlp_summed", "ones",
                             "var5", "dev5", "norm5", "turned_x", "xt_kept", "xn_kept"):
                    s[name] = sem(name)

            def credits(eng, *names):
                for name in names:
                    eng.sem_inc(s[name], CREDIT)

            def done(eng, name, k):
                eng.wait_ge(s[name], k + CREDIT + 1)

            def passes(step):
                behind = (A, BB, C) if linear else (A,)

                def parts(n):
                    return [d for d in (FRONT, 0, *behind) if 0 <= n - d < QUAD]

                def run(eng):
                    first, last = len(behind), QUAD - 2
                    first += (last + 1 - first) % 2
                    for n in range(-1, first):
                        step(n, n % 2, parts(n), parts(n - 1))
                    with eng.Fori(0, (last + 1 - first) // 2) as i:
                        for n in (first, first + 1):
                            step(i * 2 + n, n % 2, parts(n), parts(n - 1))
                    for n in range(last + 1, QUAD + len(behind)):
                        step(n, n % 2, parts(n), parts(n - 1))
                return run

            def deviations(act, name, m, i):
                done(act, "var" + str(i), m)
                nc.scalar.activation(sds[:, i, :], ves[:, i, :], ACT.Sqrt).then_inc(s["dev" + str(i)], 1)

            def moments(dve, source, m, i):
                for t in range(4):
                    nc.vector.bn_stats(st6[:, t, :], source(t))
                dve.drain()
                for t in range(4):
                    nc.vector.bn_aggr(mvs[:, i, t, :], st6[:, t, :])
                dve.drain()
                nc.vector.tensor_scalar(ves[:, i, :], mvs[:, i, :, 1], EPS, None, ALU.add).then_inc(s["var" + str(i)], 1)

            def norm(dve, out_tile, in_tile, m, i):
                done(dve, "dev" + str(i), m)
                nc.vector.reciprocal(ves[:, i, :], sds[:, i, :])
                dve.drain()
                for t in range(4):
                    last = nc.vector.tensor_scalar(out_tile(t), in_tile(t), mvs[:, i, t, 0:1], ves[:, i, t:t + 1],
                                                   ALU.subtract, ALU.mult)
                last.then_inc(s["norm" + str(i)], 1)

            with nc.Block() as block:
                @block.sync
                def _(sp):
                    for e in range(E):
                        sp.dma_start(buffers["w1"][:, e, :], w1[e]).then_inc(buffers["loaded"], 16)
                        sp.dma_start(buffers["w2"][:, e, :, :], w2[e].rearrange("(c p) d -> p c d", p=P)).then_inc(buffers["loaded"], 16)

                @block.tensor
                def _(pe):
                    if linear:
                        pe.wait_ge(s_big, 16 * BIG_LOADS)
                    credits(pe, "up", "down", "turned_f", "f_product", "turned_zf", "scored", "turned_w", "bias_product", *(("turned_z", "product", "turned_o", "o_product", "turned_z2", "up2", "down2", "turned_x") if linear else ()))

                    def step(n, par, on, before_):
                        def bank_of(use):
                            reader = freed_by(use, *([p for p in parts_ if linear or p != A] for parts_ in (on, before_)))
                            if reader:
                                event, per, k, behind = reader
                                done(pe, event, (n - behind) * per + k)
                            return ring_bank(use)

                        def turned(use, source):
                            return turn(bank_of(use), lambda t: source[:, t, :])

                        for k in range(E + 1):
                            if 0 in on and k < E:
                                if k == 0:
                                    if 0 not in before_:
                                        pe.wait_ge(buffers["loaded"], 16 * 2 * E)
                                    done(pe, "htf_ready", n)
                                for c in range(FC):
                                    u = (n * E + k) * FC + c
                                    done(pe, "gelu", u - 4)
                                    nc.tensor.matmul(bank(c), w1s[:, k, c * P:(c + 1) * P], ft[:, bass.ds(n * BANK, BANK)],
                                                     start=True, stop=True).then_inc(s["up"], 1)
                            if C in on and k < 3:
                                m = n - C
                                if k == 0:
                                    done(pe, "ht_ready", m)
                                for c in MLP_CHUNKS[k]:
                                    nc.tensor.matmul(bank(bank_of("up" + str(c))), fc_s[:, c * P:(c + 1) * P], ht[:, :],
                                                     start=True, stop=True).then_inc(s["up2"], 1)
                            if C in on and k == 3:
                                done(pe, "gelu2", (n - C) * 4 + 3)
                                at = bank_of("down")
                                for t in range(4):
                                    for c in range(FC):
                                        last = nc.tensor.matmul(ps[:, at * BANK + t * P:at * BANK + (t + 1) * P],
                                                                h2[:, c, t * P:(t + 1) * P], pj_s[:, c, :],
                                                                start=c == 0, stop=c == FC - 1)
                                last.then_inc(s["down2"], 1)
                            if C in on and k == 8:
                                done(pe, "norm5", n - C)
                                turned("turn_x", zx).then_inc(s["turned_x"], 1)
                            if BB in on and k == 5:
                                done(pe, "o_made", (n - BB) * 4 + 3)
                                turned("turn_o", os_).then_inc(s["turned_o"], 1)
                            if BB in on and k == 6:
                                done(pe, "ot_ready", n - BB)
                                at = bank_of("prod_o")
                                for t in range(4):
                                    last = nc.tensor.matmul(ps[:, at * BANK + t * P:at * BANK + (t + 1) * P],
                                                            ot[:, t * P:(t + 1) * P], wo_s[:, :], start=True, stop=True)
                                last.then_inc(s["o_product"], 1)
                            if BB in on and k == 8:
                                done(pe, "norm3", n - BB)
                                turned("turn_z2", z2).then_inc(s["turned_z2"], 1)
                            if A in on and linear and k == 5:
                                done(pe, "norm2", n - A)
                                turned("turn_z", z).then_inc(s["turned_z"], 1)
                            if A in on and linear and k in (6, 7):
                                if k == 6:
                                    done(pe, "zt_ready", n - A)
                                for t in (2 * k - 12, 2 * k - 11):
                                    nc.tensor.matmul(bank(bank_of("qkv" + str(t)), 3 * D), zt[:, t * P:(t + 1) * P], wall[:, :],
                                                     start=True, stop=True).then_inc(s["product"], 1)
                            if FRONT in on:
                                m, qpar = n - FRONT, 1 - par
                                if k == 1:
                                    done(pe, "staged", m)
                                    turned("turn_f", osf).then_inc(s["turned_f"], 1)
                                if k == 2:
                                    done(pe, "otf_ready", m)
                                    at = bank_of("prod_f")
                                    for t in range(4):
                                        last = nc.tensor.matmul(ps[:, at * BANK + t * P:at * BANK + (t + 1) * P],
                                                                otf[:, t * P:(t + 1) * P], w_o_s[:, :], start=True, stop=True)
                                    last.then_inc(s["f_product"], 1)
                                if k == 4:
                                    done(pe, "norm4", m)
                                    turned("turn_zf", zf).then_inc(s["turned_zf"], 1)
                                if k == 5:
                                    done(pe, "htf_ready", m)
                                    at = bank_of("logits")
                                    for t in range(4):
                                        last = nc.tensor.matmul(ps[:, at * BANK + t * E:at * BANK + (t + 1) * E],
                                                                htf[:, t * P:(t + 1) * P], wg_s[:, :], start=True, stop=True)
                                    last.then_inc(s["scored"], 1)
                                if k == 7:
                                    done(pe, "shares", m)
                                    at = bank_of("turn_w")
                                    for t in range(4):
                                        last = nc.tensor.transpose(ps[0:E, at * BANK + t * P:at * BANK + (t + 1) * P],
                                                                   ws[:, qpar, t, :], ident)
                                    last.then_inc(s["turned_w"], 1)
                                if k == 8:
                                    done(pe, "wt_ready", m)
                                    at = bank_of("bias")
                                    for t in range(4):
                                        last = nc.tensor.matmul(ps[:, at * BANK + t * P:at * BANK + (t + 1) * P],
                                                                wt[:, t * P:(t + 1) * P], bb2s[:, :], start=True, stop=True)
                                    last.then_inc(s["bias_product"], 1)
                            if 0 in on and k:
                                e = n * E + k - 1
                                done(pe, "gelu", e * FC + 3)
                                done(pe, "summed", e - 2)
                                for t in range(4):
                                    for c in range(FC):
                                        col = (4 + (k - 1) % 2) * BANK + t * P
                                        last = nc.tensor.matmul(ps[:, col:col + P], h1[:, (k - 1) % 2, c, t * P:(t + 1) * P],
                                                                w2s[:, k - 1, c, :], start=c == 0, stop=c == FC - 1)
                                last.then_inc(s["down"], 1)

                    passes(step)(pe)

                @block.scalar
                def _(act):
                    credits(act, "gelu", "dev0", "dev4", "otf_ready", "htf_ready", "ex_ready", "wt_ready", *(("dev1", "dev2", "dev3", "zt_ready", "expd", "ot_ready", "ht_ready", "gelu2", "dev5", "xt_kept") if linear else ()))

                    def step(n, par, on, before_):
                        for k in range(E + 1):
                            if 0 in on and k < E:
                                done(act, "down", n * E + k - 2)
                                for c in range(FC):
                                    done(act, "up", (n * E + k) * FC + c)
                                    nc.scalar.activation(h1[:, k % 2, c, :], bank(c), ACT.Gelu_apprx_tanh,
                                                         bias=fcols[:, k * FC + c:k * FC + c + 1]).then_inc(s["gelu"], 1)
                            if C in on and k < 3:
                                m = n - C
                                if k == 0:
                                    done(act, "down2", m - 1)
                                for c in MLP_CHUNKS[k]:
                                    done(act, "up2", m * 4 + c)
                                    nc.scalar.activation(h2[:, c, :], bank(ring_bank("up" + str(c))), ACT.Gelu,
                                                         bias=mcols[:, 4 + c:5 + c]).then_inc(s["gelu2"], 1)
                            if C in on and k == 6:
                                deviations(act, "var5", n - C, 5)
                            if C in on and k == 8:
                                done(act, "turned_x", n - C)
                                nc.scalar.activation(ft[:, bass.ds((n - C) * BANK, BANK)], bank(ring_bank("turn_x")), ACT.Copy).then_inc(s["xt_kept"], 1)
                            if BB in on and k == 5:
                                done(act, "turned_o", n - BB)
                                done(act, "o_product", n - BB - 1)
                                nc.scalar.activation(ot[:, :], bank(ring_bank("turn_o")), ACT.Copy).then_inc(s["ot_ready"], 1)
                            if BB in on and k == 6:
                                deviations(act, "var3", n - BB, 3)
                            if BB in on and k == 8:
                                done(act, "turned_z2", n - BB)
                                done(act, "up2", (n - BB - 1) * 4 + 3)
                                nc.scalar.activation(ht[:, :], bank(ring_bank("turn_z2")), ACT.Identity, bias=mcols[:, 3:4],
                                                     scale=mcols[:, 2:3]).then_inc(s["ht_ready"], 1)
                            if A in on and k == 0:
                                deviations(act, "var0", n - A, 0)
                            if A in on and linear and k == 2:
                                deviations(act, "var1", n - A, 1)
                            if A in on and linear and k == 3:
                                deviations(act, "var2", n - A, 2)
                            if A in on and linear and k == 5:
                                done(act, "turned_z", n - A)
                                done(act, "product", (n - A - 1) * 4 + 3)
                                nc.scalar.activation(zt[:, :], bank(ring_bank("turn_z")), ACT.Identity, bias=mcols[:, 1:2],
                                                     scale=mcols[:, 0:1]).then_inc(s["zt_ready"], 1)
                            if A in on and linear and k == 7:
                                done(act, "lowered", n - A)
                                nc.scalar.activation(low[:, :, :], low[:, :, :], ACT.Exp).then_inc(s["expd"], 1)
                            if FRONT in on:
                                m = n - FRONT
                                if k == 1:
                                    done(act, "turned_f", m)
                                    done(act, "f_product", m - 1)
                                    nc.scalar.activation(otf[:, :], bank(ring_bank("turn_f")), ACT.Copy).then_inc(s["otf_ready"], 1)
                                if k == 2:
                                    deviations(act, "var4", m, 4)
                                if k == 4:
                                    done(act, "turned_zf", m)
                                    done(act, "scored", m - 1)
                                    gain, shift = fcols[:, E * FC:E * FC + 1], fcols[:, E * FC + 1:E * FC + 2]
                                    for dst in (htf[:, :], ft[:, bass.ds(m * BANK, BANK)]):
                                        last = nc.scalar.activation(dst, bank(ring_bank("turn_zf")), ACT.Identity, bias=shift, scale=gain)
                                    last.then_inc(s["htf_ready"], 1)
                                if k == 5:
                                    done(act, "centred", m)
                                    nc.scalar.activation(ex[:, :, :], ex[:, :, :], ACT.Exp).then_inc(s["ex_ready"], 1)
                                if k == 7:
                                    done(act, "turned_w", m)
                                    done(act, "bias_product", m - 1)
                                    nc.scalar.activation(wt[:, :], ps[0:E, ring_bank("turn_w") * BANK:(ring_bank("turn_w") + 1) * BANK],
                                                         ACT.Copy).then_inc(s["wt_ready"], 1)

                    passes(step)(act)

                @block.vector
                def _(dve):
                    credits(dve, "summed", "added", "var0", "norm0", "var4", "norm4", "f_summed", "centred", "shares", "prepared", *((
                        "var1", "norm1", "var2", "norm2", "var3", "norm3", "qkv_kept", "lowered", "featured", "kv_summed",
                        "weighed", "o_made", "o_summed", "mlp_summed", "var5", "norm5") if linear else ()))

                    def front(m, par, k):
                        if k == 2:
                            done(dve, "f_product", m)
                            nc.vector.tensor_tensor(tiles(xn, m), tiles(xn, m), quad(ring_bank("prod_f")), ALU.add).then_inc(s["f_summed"], 1)
                            dve.drain()
                            moments(dve, lambda t: tile(xn, m, t), m, 4)
                        if k == 3:
                            done(dve, "turned_zf", m - 1)
                            done(dve, "h_gained", m - 1)
                            norm(dve, lambda t: zf[:, t, :], lambda t: tile(xn, m, t), m, 4)
                        if k == 5:
                            done(dve, "scored", m)
                            logits = bank(ring_bank("logits"), 4 * E).rearrange("p (t e) -> p t e", t=4)
                            nc.vector.tensor_reduce(peak[:, :], logits, AX.X, ALU.max)
                            dve.drain()
                            nc.vector.tensor_tensor(ex[:, :, :], logits, each(peak), ALU.subtract).then_inc(s["centred"], 1)
                        if k == 6:
                            done(dve, "ex_ready", m)
                            nc.vector.tensor_copy(rest[:, :, :], ex[:, :, :])
                            dve.drain()
                            for t in range(4):
                                nc.vector.max(top[:, t, :], rest[:, t, :])
                            dve.drain()
                            nc.vector.memset(top[:, :, 2:8], -1.0)
                            nc.vector.tensor_tensor(total[:, :], top[:, :, 0], top[:, :, 1], ALU.add)
                            dve.drain()
                            for t in range(4):
                                nc.vector.match_replace(rest[:, t, :], top[:, t, :], ex[:, t, :], 0.0)
                            nc.vector.reciprocal(peak[:, :], total[:, :])
                            dve.drain()
                            nc.vector.tensor_tensor(ex[:, :, :], ex[:, :, :], rest[:, :, :], ALU.subtract)
                            dve.drain()
                            done(dve, "turned_w", m - 2)
                            nc.vector.tensor_tensor(ws[:, par, :, :], ex[:, :, :], each(peak), ALU.mult).then_inc(s["shares"], 1)
                        if k == 8:
                            done(dve, "h_ready", m)
                            done(dve, "bias_product", m)
                            nc.vector.tensor_tensor(acc[:, par, :, :], hs[:, :, :], quad(ring_bank("bias")), ALU.add).then_inc(s["prepared"], 1)

                    def each(column):
                        return column[:, :].rearrange("p (t a) -> p t a", a=1).to_broadcast([P, 4, E])

                    def attend(m, t):
                        k = m * 4 + t
                        done(dve, "outer", k)
                        nc.vector.tensor_reduce(kv[:, :, :].rearrange("p d e -> p (d e)"),
                                                pr1[:, t % 2, :, :, :].rearrange("p h d e -> p (d e) h"), AX.X, ALU.add).then_inc(s["kv_summed"], 1)
                        done(dve, "kv_summed", k)
                        fq = feat[:, t, 0:D].rearrange("p (h a d) -> p h a d", a=1, d=HD)
                        kvt = kv[:, :, :].rearrange("p (a d) e -> p a e d", a=1)
                        nc.vector.tensor_tensor(pr2[:, :, :, :], fq.to_broadcast([P, H, VW, HD]), kvt.to_broadcast([P, H, VW, HD]),
                                                ALU.mult).then_inc(s["weighed"], 1)
                        done(dve, "weighed", k)
                        nc.vector.tensor_reduce(res[:, :, :], pr2[:, :, :, :], AX.X, ALU.add)
                        dve.drain()
                        nc.vector.tensor_scalar(den[:, :], res[:, :, HD], 1e-6, None, ALU.add)
                        dve.drain()
                        nc.vector.reciprocal(den[:, :], den[:, :])
                        dve.drain()
                        if t == 0:
                            done(dve, "turned_o", m - 1)
                        nc.vector.tensor_tensor(os_[:, t, :].rearrange("p (h e) -> p h e", h=H), res[:, :, 0:HD],
                                                den[:, :].rearrange("p (h a) -> p h a", a=1).to_broadcast([P, H, HD]),
                                                ALU.mult).then_inc(s["o_made"], 1)

                    def step(n, par, on, before_):
                        for k in range(E + 1):
                            if BB in on and k == 6:
                                m = n - BB
                                done(dve, "o_product", m)
                                nc.vector.tensor_tensor(tiles(xn, m), tiles(xn, m), quad(ring_bank("prod_o")), ALU.add).then_inc(s["o_summed"], 1)
                                done(dve, "o_summed", m)
                                nc.vector.tensor_tensor(tiles(xn, m), tiles(xn, m), wide(mrows[:, 3 * D:4 * D]), ALU.add)
                                dve.drain()
                                moments(dve, lambda t: tile(xn, m, t), m, 3)
                            if BB in on and k == 7:
                                m = n - BB
                                done(dve, "turned_z2", m - 1)
                                norm(dve, lambda t: z2[:, t, :], lambda t: tile(xn, m, t), m, 3)
                            if A in on:
                                m = n - A
                                if k == 0:
                                    done(dve, "summed", m * E + E - 1)
                                    moments(dve, lambda t: acc[:, 1 - par, t, :], m, 0)
                                if k == 1:
                                    done(dve, "gained", m - 1)
                                    norm(dve, lambda t: ze[:, t, :], lambda t: acc[:, 1 - par, t, :], m, 0)
                                if k == 2:
                                    done(dve, "shifted", m)
                                    nc.vector.tensor_tensor(tiles(x, m), tiles(x, m), fs[:, :, :], ALU.add).then_inc(s["added"], 1)
                                    if linear:
                                        dve.drain()
                                        moments(dve, lambda t: tile(x, m, t), m, 1)
                            if A in on and linear:
                                if k == 3:
                                    norm(dve, lambda t: tile(xn, m, t), lambda t: tile(x, m, t), m, 1)
                                    dve.drain()
                                    moments(dve, lambda t: tile(xn, m, t), m, 2)
                                if k == 4:
                                    done(dve, "turned_z", m - 1)
                                    norm(dve, lambda t: z[:, t, :], lambda t: tile(xn, m, t), m, 2)
                                if k in (6, 7):
                                    for t in (2 * k - 12, 2 * k - 11):
                                        at = ring_bank("qkv" + str(t)) * BANK
                                        done(dve, "product", m * 4 + t)
                                        nc.vector.tensor_tensor(qk[:, t, :], ps[:, at:at + 2 * D], mrows[:, 0:2 * D], ALU.add)
                                        done(dve, "outer", (m - 1) * 4 + t)
                                        nc.vector.tensor_tensor(vx[:, t, :, 0:HD],
                                                                ps[:, at + 2 * D:at + 3 * D].rearrange("p (h e) -> p h e", h=H),
                                                                mrows[:, 2 * D:3 * D].rearrange("p (h e) -> p h e", h=H),
                                                                ALU.add).then_inc(s["qkv_kept"], 1)
                                if k == 7:
                                    done(dve, "qkv_kept", m * 4 + 3)
                                    done(dve, "featured", m - 1)
                                    nc.vector.tensor_scalar(low[:, :, :], qk[:, :, :], 0.0, None, ALU.min).then_inc(s["lowered"], 1)
                                if k == 8:
                                    done(dve, "expd", m)
                                    done(dve, "weighed", (m - 1) * 4 + 3)
                                    nc.vector.scalar_tensor_tensor(feat[:, :, :], qk[:, :, :], 0.0, low[:, :, :], ALU.max,
                                                                   ALU.add).then_inc(s["featured"], 1)
                            if FRONT in on:
                                front(n - FRONT, 1 - par, k)
                            if C in on and k == 4:
                                m = n - C
                                done(dve, "down2", m)
                                nc.vector.tensor_tensor(ys[:, :, :], tiles(xn, m), quad(ring_bank("down")), ALU.add).then_inc(s["mlp_summed"], 1)
                                done(dve, "mlp_summed", m)
                                nc.vector.tensor_tensor(ys[:, :, :], ys[:, :, :], wide(mrows[:, 4 * D:5 * D]), ALU.add)
                                dve.drain()
                                nc.vector.tensor_tensor(tiles(x, m), tiles(x, m), ys[:, :, :], ALU.add)
                                dve.drain()
                                moments(dve, lambda t: tile(x, m, t), m, 5)
                            if BB in on and k < 4:
                                attend(n - BB, k)
                            if C in on and k == 7:
                                m = n - C
                                done(dve, "turned_x", m - 1)
                                done(dve, "xn_kept", m - 1)
                                norm(dve, lambda t: zx[:, t, :], lambda t: tile(x, m, t), m, 5)
                            if 0 in on and k:
                                e = n * E + k - 1
                                if k == 1:
                                    done(dve, "prepared", n)
                                done(dve, "summed", e - 1)
                                done(dve, "down", e)
                                for t in range(4):
                                    col = (4 + (k - 1) % 2) * BANK + t * P
                                    last = nc.vector.scalar_tensor_tensor(
                                        acc[:, par, t, :], ps[:, col:col + P], ws[:, par, t, k - 1:k], acc[:, par, t, :],
                                        ALU.mult, ALU.add)
                                last.then_inc(s["summed"], 1)

                    passes(step)(dve)

                @block.gpsimd
                def _(pool):
                    credits(pool, "staged", "h_gained", "h_ready", "gained", "shifted", *(("outer", "xn_kept") if linear else ()))
                    if linear:
                        nc.gpsimd.memset(vx[:, :, :, HD:VW], 1.0).then_inc(s["ones"], 1)
                        pool.wait_ge(s["ones"], 1)

                    def step(n, par, on, before_):
                        if FRONT in on:
                            done(pool, "turned_f", n - FRONT - 1)
                            nc.gpsimd.tensor_copy(osf[:, :, :], tiles(o, n - FRONT)).then_inc(s["staged"], 1)
                        for t in range(4):
                            if BB in on:
                                m = n - BB
                                done(pool, "featured", m)
                                done(pool, "kv_summed", m * 4 + t - 2)
                                fk = feat[:, t, D:2 * D].rearrange("p (h d a) -> p h d a", h=H, a=1)
                                v = vx[:, t, :, :].rearrange("p h (a e) -> p h a e", a=1)
                                nc.gpsimd.tensor_tensor(pr1[:, t % 2, :, :, :], fk.to_broadcast([P, H, HD, VW]),
                                                        v.to_broadcast([P, H, HD, VW]), ALU.mult).then_inc(s["outer"], 1)
                            if A in on and t == 1:
                                m = n - A
                                done(pool, "norm0", m)
                                done(pool, "shifted", m - 1)
                                nc.gpsimd.tensor_tensor(gs[:, :, :], ze[:, :, :], wide(rows[:, 2, :]), ALU.mult).then_inc(s["gained"], 1)
                                done(pool, "gained", m)
                                done(pool, "added", m - 1)
                                nc.gpsimd.tensor_tensor(fs[:, :, :], gs[:, :, :], wide(rows[:, 3, :]), ALU.add).then_inc(s["shifted"], 1)
                        if FRONT in on:
                            m = n - FRONT
                            done(pool, "norm4", m)
                            done(pool, "prepared", m - 1)
                            nc.gpsimd.tensor_tensor(hs[:, :, :], zf[:, :, :], wide(rows[:, 0, :]), ALU.mult).then_inc(s["h_gained"], 1)
                            done(pool, "h_gained", m)
                            nc.gpsimd.tensor_tensor(hs[:, :, :], hs[:, :, :], wide(rows[:, 1, :]), ALU.add).then_inc(s["h_ready"], 1)
                        if C in on:
                            done(pool, "norm5", n - C)
                            nc.gpsimd.tensor_copy(tiles(xn, n - C), zx[:, :, :]).then_inc(s["xn_kept"], 1)

                    passes(step)(pool)

        buffers = {}
        ffn("f1")
        ffn("f2")
        s_out = sem("out_stored")
        with nc.Block() as block:
            @block.sync
            def _(sp):
                sp.dma_start(out.rearrange("b (t p) d -> p (b t) d", p=P), x[:, :, :]).then_inc(s_out, 16)
                sp.wait_ge(s_out, 16)


def constants():
    i = np.arange(P)
    row = i % STRIP
    c = np.zeros((P, 2 * P + 4), np.float32)
    c[:, 0:P] = np.eye(P)
    c[:, P:2 * P] = np.where(i[None, :] > i[:, None], NEG, 0)
    c[:, 2 * P] = np.where((row >= 2 * HD) & (row < 3 * HD), -1, 0)
    c[:, 2 * P + 1] = np.where((row >= HD) & (row < 2 * HD), -1, 0)
    c[:, 2 * P + 2] = row == ONE_ROW
    c[:, 2 * P + 3] = 1
    return c


_INS = ['L0_attn_q_x', 'L0_attn_ln1_w', 'L0_attn_ln1_b', 'L0_attn_wq', 'L0_attn_bq', 'L0_attn_wk', 'L0_attn_bk',
        'L0_attn_wv', 'L0_attn_bv', 'L0_attn_wo', 'L0_attn_bo', 'L0_attn_ln2_w', 'L0_attn_ln2_b', 'L0_attn_fc_w',
        'L0_attn_fc_b', 'L0_attn_proj_w', 'L0_attn_proj_b', 'L0_ffn_w_qkv', 'L0_ffn_w_o', 'L0_ffn_g1', 'L0_ffn_b1',
        'L0_ffn_wg', 'L0_ffn_w1', 'L0_ffn_bb1', 'L0_ffn_w2', 'L0_ffn_bb2', 'L0_ffn_g2', 'L0_ffn_b2']


def kernel(**inputs):
    import concourse.bacc as _bacc
    from concourse.bass_utils import run_bass_kernel_spmd as _run

    nc = _bacc.Bacc("TRN2", target_bir_lowering=False, num_devices=1)
    arrays, args = {}, []
    for name in _INS:
        a = np.ascontiguousarray(inputs[name])
        arrays[f"in_{name}"] = a
        args.append(nc.dram_tensor(f"in_{name}", a.shape, mybir.dt.from_np(a.dtype), kind="ExternalInput").ap())
    arrays["constants"] = constants()
    args.append(nc.dram_tensor("constants", arrays["constants"].shape, F32, kind="ExternalInput").ap())
    args.append(nc.dram_tensor("out_dram", (B, N, D), F32, kind="ExternalOutput").ap())
    program(nc, *args)
    r = _run(nc, [arrays], core_ids=[0])
    return r.results[0]["out_dram"]
```
